# Optimizing a Trainium2 kernel written in Bass

```python
import numpy as np
import jax
import jax.numpy as jnp

def _softmax(x, axis=-1):
    return jax.nn.softmax(x, axis=axis)

def _gelu(x):
    return jax.nn.gelu(x, approximate=True)

def _silu(x):
    return jax.nn.silu(x)

def _sigmoid(x):
    return jax.nn.sigmoid(x)

def _layernorm(x, axis=-1, eps=1e-05):
    m = jnp.mean(x, axis=axis, keepdims=True)
    v = jnp.var(x, axis=axis, keepdims=True)
    return (x - m) / jnp.sqrt(v + eps)

def _scatter_add(tgt, idx, src, axis=0):
    return tgt.at[idx].add(src)

def _segment_sum(src, seg, n):
    return jax.ops.segment_sum(src, seg, n)
kernel_name = 'mk_perceiver_d1_seqx_r4_3c84a5'

def setup_inputs(seed: int=0):
    np.random.seed(seed)
    _w = jnp.asarray

    def _rec_inputs():
        import jax
        import jax.numpy as jnp
        _rk = jax.random.key(seed)
        x = -0.0002928 + 1 * jax.random.normal(jax.random.fold_in(_rk, 1), (1, 128, 256), jnp.float32)
        _lenS = 128 - jax.random.randint(jax.random.fold_in(_rk, 7), (1,), 0, max(1, 128 // 4) + 1, jnp.int32)
        _lenS2 = 12544 - jax.random.randint(jax.random.fold_in(_rk, 8), (1,), 0, max(1, 12544 // 4) + 1, jnp.int32)
        _ctx_1024P = jax.random.normal(jax.random.fold_in(_rk, 11), (1, 16, 256), jnp.float32)
        _ctx_1024c = jax.random.dirichlet(jax.random.fold_in(_rk, 511), 0.3 * jnp.ones((16,), jnp.float32), (1, 12544))
        _ctx_1024t = jnp.einsum('bsk,bkd->bsd', _ctx_1024c, _ctx_1024P)
        _ctx_1024t = _ctx_1024t * jax.lax.rsqrt(jnp.mean(jnp.square(_ctx_1024t)) + 1e-12) * 0.953939
        ctx_1024 = 4.13588e-05 + 0.999923 * (_ctx_1024t + 0.3 * jax.random.normal(jax.random.fold_in(_rk, 611), (1, 12544, 256), jnp.float32))
        return (x, ctx_1024)
    x, ctx_1024 = _rec_inputs()

    def _L0_xattn_setup():
        import jax, jax.numpy as jnp
        import numpy as np
        HIDDEN = 256
        NUM_HEADS = 16
        HEAD_DIM = HIDDEN // NUM_HEADS
        SCALE = 1.0 / float(np.sqrt(HEAD_DIM))
        key = jax.random.key(seed)
        ks = jax.random.split(key, 10)
        B, SQ, SKV = (2, 512, 1024)
        init = 0.02
        return {'query_states': jax.random.normal(ks[0], (B, SQ, HIDDEN), dtype=jnp.float32), 'key_value_states': jax.random.normal(ks[1], (B, SKV, HIDDEN), dtype=jnp.float32), 'Wq': jax.random.normal(ks[2], (HIDDEN, HIDDEN), dtype=jnp.float32) * init, 'bq': jnp.zeros((HIDDEN,), dtype=jnp.float32), 'Wk': jax.random.normal(ks[3], (HIDDEN, HIDDEN), dtype=jnp.float32) * init, 'bk': jnp.zeros((HIDDEN,), dtype=jnp.float32), 'Wv': jax.random.normal(ks[4], (HIDDEN, HIDDEN), dtype=jnp.float32) * init, 'bv': jnp.zeros((HIDDEN,), dtype=jnp.float32), 'Wo': jax.random.normal(ks[5], (HIDDEN, HIDDEN), dtype=jnp.float32) * init, 'bo': jnp.zeros((HIDDEN,), dtype=jnp.float32)}
    _L0_xattn_all = _L0_xattn_setup()
    _L0_xattn_in = {k: v for k, v in _L0_xattn_all.items() if k in ('Wq', 'bq', 'Wk', 'bk', 'Wv', 'bv', 'Wo', 'bo')}
    del _L0_xattn_all

    def _L0_attn_setup():
        import jax, jax.numpy as jnp
        import numpy as np
        DIM = 256
        HEADS = 16
        HEAD_DIM = DIM // HEADS

        def feature_map(x):
            return jnp.where(x > 0, x + 1.0, jnp.exp(x))
        key = jax.random.key(seed)
        ks = jax.random.split(key, 11)
        B, N, D = (4, 2048, DIM)
        s = 1.0 / np.sqrt(D)
        inp = {'x': jax.random.normal(ks[0], (B, N, D), dtype=jnp.float32), 'wg_w': jax.random.normal(ks[1], (D, D), dtype=jnp.float32) * s, 'wg_b': jnp.zeros((D,), dtype=jnp.float32), 'wq_w': jax.random.normal(ks[2], (D, D), dtype=jnp.float32) * s, 'wq_b': jnp.zeros((D,), dtype=jnp.float32), 'wk_w': jax.random.normal(ks[3], (D, D), dtype=jnp.float32) * s, 'wk_b': jnp.zeros((D,), dtype=jnp.float32), 'wv_w': jax.random.normal(ks[4], (D, D), dtype=jnp.float32) * s, 'wv_b': jnp.zeros((D,), dtype=jnp.float32), 'out_w': jax.random.normal(ks[5], (D, D), dtype=jnp.float32) * s, 'out_b': jnp.zeros((D,), dtype=jnp.float32)}
        return inp
    _L0_attn_all = _L0_attn_setup()
    _L0_attn_in = {k: v for k, v in _L0_attn_all.items() if k in ('wg_w', 'wg_b', 'wq_w', 'wq_b', 'wk_w', 'wk_b', 'wv_w', 'wv_b', 'out_w', 'out_b')}
    del _L0_attn_all

    def _L0_ffn_setup():
        import jax, jax.numpy as jnp
        import numpy as np
        H = 256
        I = 512
        NH = 16
        HD = H // NH
        E = 8
        TOPK = 2
        MAX_SEQ = 512
        EPS = 1e-06
        NEG = -1000000000.0

        def precompute_freqs_cis(dim, max_seq_len, theta=10000.0):
            pos = np.arange(max_seq_len, dtype=np.float32)
            freqs = np.arange(0, dim, 2, dtype=np.float32) / dim
            inv_freq = 1.0 / theta ** freqs
            f = np.einsum('i,j->ij', pos, inv_freq)
            return jnp.asarray(np.concatenate([np.cos(f), np.sin(f)], axis=-1), dtype=jnp.float32)

        def rmsnorm(x, w):
            rms = jnp.sqrt(jnp.mean(x * x, axis=-1, keepdims=True) + EPS)
            return w * (x / rms)

        def apply_rope(x, freqs_cis):
            B, S, nh, hd = x.shape
            xr = x.reshape(B, S, nh, hd // 2, 2)
            fr = freqs_cis[:S].reshape(1, S, 1, hd // 2, 2)
            a, b = (xr[..., 0], xr[..., 1])
            cr, ci = (fr[..., 0], fr[..., 1])
            out = jnp.stack([a * cr - b * ci, a * ci + b * cr], axis=-1)
            return out.reshape(B, S, nh, hd)

        def attention(x, wq, wk, wv, wo, freqs_cis):
            B, S, _ = x.shape
            q = (x @ wq).reshape(B, S, NH, HD)
            k = (x @ wk).reshape(B, S, NH, HD)
            v = (x @ wv).reshape(B, S, NH, HD)
            q = apply_rope(q, freqs_cis)
            k = apply_rope(k, freqs_cis)
            scores = jnp.einsum('bqhd,bkhd->bhqk', q, k) / np.sqrt(HD).astype(np.float32)
            causal = jnp.tril(jnp.ones((S, S), dtype=bool))
            scores = jnp.where(causal[None, None], scores, NEG)
            attn = jax.nn.softmax(scores, axis=-1)
            out = jnp.einsum('bhqk,bkhd->bqhd', attn, v).reshape(B, S, H)
            return out @ wo

        def moe_ffn(x, router_w, w1, w2, w3):
            B, S, _ = x.shape
            xt = x.reshape(B * S, H)
            logits = xt @ router_w
            probs = jax.nn.softmax(logits, axis=-1)
            topv, topi = jax.lax.top_k(probs, TOPK)
            topv = topv / jnp.sum(topv, axis=-1, keepdims=True)
            combine = jnp.sum(topv[..., None] * jax.nn.one_hot(topi, E, dtype=xt.dtype), axis=1)
            h1 = jnp.einsum('th,ehi->eti', xt, w1)
            h3 = jnp.einsum('th,ehi->eti', xt, w3)
            ye = jnp.einsum('eti,eih->eth', jax.nn.silu(h1) * h3, w2)
            out = jnp.einsum('te,eth->th', combine, ye)
            return out.reshape(B, S, H)
        key = jax.random.key(seed)
        ks = jax.random.split(key, 12)
        B, S = (2, 256)
        s = lambda fan: 1.0 / np.sqrt(fan)
        inp = {'x': jax.random.normal(ks[0], (B, S, H), dtype=jnp.float32), 'attn_norm_w': jnp.ones((H,), dtype=jnp.float32), 'ffn_norm_w': jnp.ones((H,), dtype=jnp.float32), 'wq': jax.random.normal(ks[1], (H, H), dtype=jnp.float32) * s(H), 'wk': jax.random.normal(ks[2], (H, H), dtype=jnp.float32) * s(H), 'wv': jax.random.normal(ks[3], (H, H), dtype=jnp.float32) * s(H), 'wo': jax.random.normal(ks[4], (H, H), dtype=jnp.float32) * s(H), 'router_w': jax.random.normal(ks[5], (H, E), dtype=jnp.float32) * s(H), 'w1': jax.random.normal(ks[6], (E, H, I), dtype=jnp.float32) * s(H), 'w3': jax.random.normal(ks[7], (E, H, I), dtype=jnp.float32) * s(H), 'w2': jax.random.normal(ks[8], (E, I, H), dtype=jnp.float32) * s(I), 'freqs_cis': precompute_freqs_cis(HD, MAX_SEQ)}
        return inp
    _L0_ffn_all = _L0_ffn_setup()
    _L0_ffn_in = {k: v for k, v in _L0_ffn_all.items() if k in ('attn_norm_w', 'ffn_norm_w', 'wq', 'wk', 'wv', 'wo', 'router_w', 'w1', 'w3', 'w2', 'freqs_cis')}
    del _L0_ffn_all
    return {'x': x, 'ctx_1024': ctx_1024, 'L0_xattn_Wq': _L0_xattn_in['Wq'], 'L0_xattn_bq': _L0_xattn_in['bq'], 'L0_xattn_Wk': _L0_xattn_in['Wk'], 'L0_xattn_bk': _L0_xattn_in['bk'], 'L0_xattn_Wv': _L0_xattn_in['Wv'], 'L0_xattn_bv': _L0_xattn_in['bv'], 'L0_xattn_Wo': _L0_xattn_in['Wo'], 'L0_xattn_bo': _L0_xattn_in['bo'], 'L0_attn_wg_w': _L0_attn_in['wg_w'], 'L0_attn_wg_b': _L0_attn_in['wg_b'], 'L0_attn_wq_w': _L0_attn_in['wq_w'], 'L0_attn_wq_b': _L0_attn_in['wq_b'], 'L0_attn_wk_w': _L0_attn_in['wk_w'], 'L0_attn_wk_b': _L0_attn_in['wk_b'], 'L0_attn_wv_w': _L0_attn_in['wv_w'], 'L0_attn_wv_b': _L0_attn_in['wv_b'], 'L0_attn_out_w': _L0_attn_in['out_w'], 'L0_attn_out_b': _L0_attn_in['out_b'], 'L0_ffn_attn_norm_w': _L0_ffn_in['attn_norm_w'], 'L0_ffn_ffn_norm_w': _L0_ffn_in['ffn_norm_w'], 'L0_ffn_wq': _L0_ffn_in['wq'], 'L0_ffn_wk': _L0_ffn_in['wk'], 'L0_ffn_wv': _L0_ffn_in['wv'], 'L0_ffn_wo': _L0_ffn_in['wo'], 'L0_ffn_router_w': _L0_ffn_in['router_w'], 'L0_ffn_w1': _L0_ffn_in['w1'], 'L0_ffn_w3': _L0_ffn_in['w3'], 'L0_ffn_w2': _L0_ffn_in['w2'], 'L0_ffn_freqs_cis': _L0_ffn_in['freqs_cis']}

def reference(x, ctx_1024, L0_xattn_Wq, L0_xattn_bq, L0_xattn_Wk, L0_xattn_bk, L0_xattn_Wv, L0_xattn_bv, L0_xattn_Wo, L0_xattn_bo, L0_attn_wg_w, L0_attn_wg_b, L0_attn_wq_w, L0_attn_wq_b, L0_attn_wk_w, L0_attn_wk_b, L0_attn_wv_w, L0_attn_wv_b, L0_attn_out_w, L0_attn_out_b, L0_ffn_attn_norm_w, L0_ffn_ffn_norm_w, L0_ffn_wq, L0_ffn_wk, L0_ffn_wv, L0_ffn_wo, L0_ffn_router_w, L0_ffn_w1, L0_ffn_w3, L0_ffn_w2, L0_ffn_freqs_cis):
    import jax
    import jax.numpy as jnp

    def _L0_xattn_ref(query_states, key_value_states, Wq, bq, Wk, bk, Wv, bv, Wo, bo):
        import jax, jax.numpy as jnp
        import numpy as np
        HIDDEN = 256
        NUM_HEADS = 16
        HEAD_DIM = HIDDEN // NUM_HEADS
        SCALE = 1.0 / float(np.sqrt(HEAD_DIM))
        B, SQ, _ = query_states.shape
        _, SKV, _ = key_value_states.shape
        q = query_states @ Wq.T + bq
        k = key_value_states @ Wk.T + bk
        v = key_value_states @ Wv.T + bv
        q = q.reshape(B, SQ, NUM_HEADS, HEAD_DIM).transpose(0, 2, 1, 3) * SCALE
        k = k.reshape(B, SKV, NUM_HEADS, HEAD_DIM).transpose(0, 2, 1, 3)
        v = v.reshape(B, SKV, NUM_HEADS, HEAD_DIM).transpose(0, 2, 1, 3)
        scores = jnp.einsum('bhqd,bhkd->bhqk', q, k)
        attn = jax.nn.softmax(scores, axis=-1)
        ctx = jnp.einsum('bhqk,bhkd->bhqd', attn, v)
        ctx = ctx.transpose(0, 2, 1, 3).reshape(B, SQ, HIDDEN)
        return ctx @ Wo.T + bo

    def _L0_attn_ref(x, wg_w, wg_b, wq_w, wq_b, wk_w, wk_b, wv_w, wv_b, out_w, out_b):
        import jax, jax.numpy as jnp
        import numpy as np
        DIM = 256
        HEADS = 16
        HEAD_DIM = DIM // HEADS

        def feature_map(x):
            return jnp.where(x > 0, x + 1.0, jnp.exp(x))
        B, N, D = x.shape
        H, Hd = (HEADS, HEAD_DIM)
        q = (x @ wq_w + wq_b).reshape(B, N, H, Hd)
        k = (x @ wk_w + wk_b).reshape(B, N, H, Hd)
        v = (x @ wv_w + wv_b).reshape(B, N, H, Hd)
        gate = jax.nn.sigmoid(x @ wg_w + wg_b)
        q = feature_map(q)
        k = feature_map(k)
        kv = jnp.einsum('bnhd,bnhe->bhde', k, v)
        z = 1.0 / (jnp.einsum('bnhd,bhd->bnh', q, k.sum(axis=1)) + 1e-06)
        scores = jnp.einsum('bnhd,bhde,bnh->bnhe', q, kv, z)
        out = scores.reshape(B, N, D)
        return gate * out @ out_w + out_b

    def _L0_ffn_ref(x, attn_norm_w, ffn_norm_w, wq, wk, wv, wo, router_w, w1, w3, w2, freqs_cis):
        import jax, jax.numpy as jnp
        import numpy as np
        H = 256
        I = 512
        NH = 16
        HD = H // NH
        E = 8
        TOPK = 2
        MAX_SEQ = 512
        EPS = 1e-06
        NEG = -1000000000.0

        def precompute_freqs_cis(dim, max_seq_len, theta=10000.0):
            pos = np.arange(max_seq_len, dtype=np.float32)
            freqs = np.arange(0, dim, 2, dtype=np.float32) / dim
            inv_freq = 1.0 / theta ** freqs
            f = np.einsum('i,j->ij', pos, inv_freq)
            return jnp.asarray(np.concatenate([np.cos(f), np.sin(f)], axis=-1), dtype=jnp.float32)

        def rmsnorm(x, w):
            rms = jnp.sqrt(jnp.mean(x * x, axis=-1, keepdims=True) + EPS)
            return w * (x / rms)

        def apply_rope(x, freqs_cis):
            B, S, nh, hd = x.shape
            xr = x.reshape(B, S, nh, hd // 2, 2)
            fr = freqs_cis[:S].reshape(1, S, 1, hd // 2, 2)
            a, b = (xr[..., 0], xr[..., 1])
            cr, ci = (fr[..., 0], fr[..., 1])
            out = jnp.stack([a * cr - b * ci, a * ci + b * cr], axis=-1)
            return out.reshape(B, S, nh, hd)

        def attention(x, wq, wk, wv, wo, freqs_cis):
            B, S, _ = x.shape
            q = (x @ wq).reshape(B, S, NH, HD)
            k = (x @ wk).reshape(B, S, NH, HD)
            v = (x @ wv).reshape(B, S, NH, HD)
            q = apply_rope(q, freqs_cis)
            k = apply_rope(k, freqs_cis)
            scores = jnp.einsum('bqhd,bkhd->bhqk', q, k) / np.sqrt(HD).astype(np.float32)
            causal = jnp.tril(jnp.ones((S, S), dtype=bool))
            scores = jnp.where(causal[None, None], scores, NEG)
            attn = jax.nn.softmax(scores, axis=-1)
            out = jnp.einsum('bhqk,bkhd->bqhd', attn, v).reshape(B, S, H)
            return out @ wo

        def moe_ffn(x, router_w, w1, w2, w3):
            B, S, _ = x.shape
            xt = x.reshape(B * S, H)
            logits = xt @ router_w
            probs = jax.nn.softmax(logits, axis=-1)
            topv, topi = jax.lax.top_k(probs, TOPK)
            topv = topv / jnp.sum(topv, axis=-1, keepdims=True)
            combine = jnp.sum(topv[..., None] * jax.nn.one_hot(topi, E, dtype=xt.dtype), axis=1)
            h1 = jnp.einsum('th,ehi->eti', xt, w1)
            h3 = jnp.einsum('th,ehi->eti', xt, w3)
            ye = jnp.einsum('eti,eih->eth', jax.nn.silu(h1) * h3, w2)
            out = jnp.einsum('te,eth->th', combine, ye)
            return out.reshape(B, S, H)
        h = x + attention(rmsnorm(x, attn_norm_w), wq, wk, wv, wo, freqs_cis)
        out = h + moe_ffn(rmsnorm(h, ffn_norm_w), router_w, w1, w2, w3)
        return out
    x = x + _L0_xattn_ref(_layernorm(x, axis=-1), ctx_1024, L0_xattn_Wq, L0_xattn_bq, L0_xattn_Wk, L0_xattn_bk, L0_xattn_Wv, L0_xattn_bv, L0_xattn_Wo, L0_xattn_bo)
    x = x + _L0_attn_ref(_layernorm(x, axis=-1), L0_attn_wg_w, L0_attn_wg_b, L0_attn_wq_w, L0_attn_wq_b, L0_attn_wk_w, L0_attn_wk_b, L0_attn_wv_w, L0_attn_wv_b, L0_attn_out_w, L0_attn_out_b)
    x = x + _L0_ffn_ref(_layernorm(x, axis=-1), L0_ffn_attn_norm_w, L0_ffn_ffn_norm_w, L0_ffn_wq, L0_ffn_wk, L0_ffn_wv, L0_ffn_wo, L0_ffn_router_w, L0_ffn_w1, L0_ffn_w3, L0_ffn_w2, L0_ffn_freqs_cis)
    return x

_drawn_inputs = setup_inputs


def setup_inputs(seed=0):
    import zlib

    import numpy as np

    out = dict(_drawn_inputs(seed))
    spreads = {'L0_xattn_bq': (0.0, 0.8),
     'L0_xattn_bk': (0.0, 0.8),
     'L0_xattn_bv': (0.0, 0.1),
     'L0_xattn_bo': (0.0, 0.1),
     'L0_attn_wg_b': (0.0, 0.495),
     'L0_attn_wq_b': (0.0, 0.8),
     'L0_attn_wk_b': (0.0, 0.8),
     'L0_attn_wv_b': (0.0, 0.1),
     'L0_attn_out_b': (0.0, 0.1),
     'L0_ffn_attn_norm_w': (1.0, 0.2),
     'L0_ffn_ffn_norm_w': (1.0, 0.2)}
    factors = {'L0_xattn_Wq': 3.867, 'L0_xattn_Wk': 2.915, 'L0_attn_wq_w': 2.932}
    for name, (base, spread) in spreads.items():
        noise = np.random.default_rng([zlib.crc32(name.encode()), seed]).standard_normal(out[name].shape)
        drawn = base * np.exp(spread * noise) if base else spread * noise
        out[name] = jnp.asarray(drawn.astype(out[name].dtype))
    for name, factor in factors.items():
        out[name] = (out[name] * factor).astype(out[name].dtype)
    return out
```

```python
from contextlib import ExitStack

import concourse.bass as bass
from concourse import mybir

F32 = mybir.dt.float32
F32R = mybir.dt.float32r
I32 = mybir.dt.int32
ALU = mybir.AluOpType
ACT = mybir.ActivationFunctionType
AX_X = mybir.AxisListType.X

P = 128
D = 256
DC = D // P
H = 16
HD = D // H
VW = HD + 1
PAIRS = H // 2
KEYS = 12544
BLOCKS = 7
CHUNKS = KEYS // P // BLOCKS
STEPS = CHUNKS // 2
HALF = CHUNKS // 2
GROUPS = 4
GH = H // GROUPS
EXPERTS = 8
INNER = 512
IC = INNER // P
SCALE = 0.25
MASKED = -4.0e9
EPS_LN, EPS_RMS, EPS_Z = 1e-5, 1e-6, 1e-6

WEIGHTS = ["xq", "xk", "xv", "xo", "aq", "ak", "av", "ag", "ao", "fq", "fk", "fv", "fo"]
BIASES = ["bxq", "bxk", "bxv", "bxo", "baq", "bak", "bav", "bag", "bao", "anw", "fnw"]
C_ID, C_BM, C_CA, C_HM, C_MM, C_LT = 0, 128, 256, 384, 392, 408
C_N = C_LT + EXPERTS * EXPERTS

COUNTING = [
    "ch_ready",
    "cl_ready",
    "kv_done",
    "kvf_ready",
    "kh_ready",
    "kl_ready",
    "val_ready",
    "kt_done",
    "kt_ready",
    "mx_done",
    "mx_read",
    "curmax_ready",
    "mparts_ready",
    "mt_done",
    "qmat_ready",
    "bmax_ready",
    "sc_done",
    "exp_ready",
    "pv_done",
    "part_ready",
]
ONCE = [
    "pool_setup", "dve_ident", "dve_pvzero", "act_wkvh", "dve_wkvl",
    "dve_xn", "pe_xnT", "dve_xnT", "pe_q", "dve_qparts", "pe_qT", "dve_qmat", "act_qmat",
    "dve_dmax", "act_bw", "pe_partT", "dve_partT_read",
    "dve_att", "pe_attT", "dve_attT", "pe_xo",
    "dve_a_xn", "pe_a_xnT", "dve_a_xnT", "pe_a_proj", "dve_a_neg", "act_a_exp", "dve_a_qkv",
    "pe_a_qT", "pe_a_kv", "dve_a_kvr", "pe_a_num", "dve_a_out", "pe_a_outT", "dve_a_outT", "pe_a_o",
    "dve_c_xn", "pe_c_xnT", "dve_c_xnT", "pe_c_proj", "dve_c_qk", "pe_c_qkT", "dve_c_kbd",
    "pe_c_scores", "dve_c_sub", "act_c_exp", "pe_c_pT", "dve_c_pT", "act_c_pT", "pe_c_pv",
    "dve_c_oT", "pe_c_o", "dve_c_att", "pe_c_attT", "dve_c_attT", "pe_c_proj_o",
    "dve_m_t", "pe_m_tT", "dve_m_tT", "pe_m_logits", "dve_m_sub", "act_m_exp", "dve_m_w",
    "pe_m_h", "act_m_sig", "dve_m_g", "pe_m_gT", "act_m_gT", "pe_m_down", "pe_m_all",
    "dve_fin",
]
LOADS = ["ld_x", "ld_const", "ld_q", "ld_kv", "ld_ctx0", "ld_ctx1", "ld_small", "ld_experts0",
         "ld_experts1", "ld_experts2", "ld_experts3", "experts_loaded", "stored"]


def perceiver_layer(nc, dr, out):
    ctx = ExitStack()
    with ctx:
        def sb(name, shape, dt=F32):
            return ctx.enter_context(nc.sbuf_tensor(name, shape, dt))

        S = {n: ctx.enter_context(nc.semaphore(n)) for n in COUNTING + ONCE + LOADS + ["dve_chain"]}

        x = sb("x_in", [P, D])
        w = {n: sb("w_" + n, [P, DC, D]) for n in WEIGHTS}
        router = sb("router", [P, DC, EXPERTS])
        bias = sb("bias", [P, len(BIASES), D])
        const = sb("const", [P, C_N])
        freqs = sb("freqs", [P, HD])
        ident_r = sb("ident_r", [P, P], F32R)
        ones = sb("ones", [P, 1])
        parts = sb("parts", [P, BLOCKS, GROUPS * P])
        bmax = sb("bmax", [P, BLOCKS, H])
        small = sb("small", [P, 512])
        xn = sb("xn", [P, D])
        xnT = sb("xnT", [P, DC, P])

        ARENA = 142 * 1024
        at = [(nc.sbuf_base + 31) // 32 * 32]
        arena_end = at[0] + ARENA
        sb("arena", [P, ARENA // 4])
        arena_start = at[0]

        def place(name, shape, dt=F32):
            size = 4
            for n in shape[1:]:
                size *= n
            h = nc.alloc_sbuf_tensor_at(name, shape, dt, offset=at[0])
            at[0] += (size + 31) // 32 * 32
            assert at[0] <= arena_end, (name, at[0] - arena_end)
            return h

        kT = place("kT", [P, STEPS, PAIRS, 2 * P], F32R)
        ctxT = place("ctxT", [P, CHUNKS, DC, P])
        kparts = [place(f"kparts{i}", [P, PAIRS, P], F32R) for i in range(2)]
        val = place("val", [P, CHUNKS, H, VW])
        cparts = [place(f"cparts{i}", [P, 2, DC, P], F32R) for i in range(2)]
        wkv = place("wkv", [P, 2, DC, 2 * D], F32R)
        kvf = [place(f"kvf{i}", [P, 2, D]) for i in range(2)]
        kbias = place("kbias", [P, 2, D])
        probs = [place(f"probs{i}", [P, GH, P]) for i in range(GROUPS)]
        qmat = place("qmat", [P, H, P], F32R)
        qparts = place("qparts", [P, H, 96], F32R)
        stepmax = place("stepmax", [P, STEPS, H])
        curmax = place("curmax", [P, H])
        maxparts = place("maxparts", [P, P], F32R)

        at[0] = arena_start
        w3 = place("w3", [P, EXPERTS, DC, INNER])
        w1 = place("w1", [P, EXPERTS, DC, INNER])
        w2 = place("w2", [P, EXPERTS, IC, D])
        ta = place("ta", [P, 2 * D])
        tb = place("tb", [P, 2 * D])
        tc = place("tc", [P, 2 * D])
        sm = place("sm", [P, H, P])
        pT = place("pT", [P, H, P])
        kbd = place("kbd", [P, DC, H // DC, P])
        oT = place("oT", [P, GROUPS, P])
        vaug = place("vaug", [P, H, VW])
        kvr = place("kvr", [P, DC, P + H // DC])
        x1, x2, xl, hres = (place(n, [P, D]) for n in ("x1", "x2", "xl", "hres"))
        fin = place("fin", [P, D])
        share = place("share", [P, EXPERTS, 1])

        B = [ctx.enter_context(nc.psum_tensor(f"bank{i}", [P, 512], F32)) for i in range(8)]
        kv_bank, kt_bank, sc_bank, pv_bank = B[0:2], B[2], B[3:7], B[7]

        ident = const[:, C_ID:C_ID + P]

        def bv(first, n=1):
            i = BIASES.index(first)
            return bias[:, i:i + n, :]

        def per_head(v, n):
            return v.unsqueeze(2).broadcast_to([v.shape[0], v.shape[1], n])

        def over_heads(v, n):
            return v.unsqueeze(1).broadcast_to([v.shape[0], n, v.shape[1]])

        block = ctx.enter_context(nc.Block())

        @block.sync
        def _(sp):
            def ctx_load(b, half):
                if not isinstance(b, int) or b > 0:
                    sp.wait_ge(S["cl_ready"], b * CHUNKS - CHUNKS + HALF * (half + 1))
                sp.dma_start(ctxT[:, HALF * half:HALF * (half + 1), :, :],
                             dr["ctxT"][b, half]).then_inc(S[f"ld_ctx{half}"], 16)

            def weight(name):
                return w[name][:, :, :], dr["w_" + name].rearrange("(c p) n -> p c n", p=P)

            sp.dma_start(x[:, :], dr["x"]).then_inc(S["ld_x"], 16)
            sp.dma_start(const[:, :], dr["const"]).then_inc(S["ld_const"], 16)
            sp.dma_start(*weight("xq")).then_inc(S["ld_q"], 16)
            for n, name in enumerate(BIASES):
                sp.dma_start(bias[:, n, :], dr[name].partition_broadcast(P)).then_inc(S["ld_q"], 16)
            sp.dma_start(*weight("xk")).then_inc(S["ld_kv"], 16)
            sp.dma_start(*weight("xv")).then_inc(S["ld_kv"], 16)
            ctx_load(0, 0)
            ctx_load(0, 1)
            for name in WEIGHTS[3:]:
                sp.dma_start(*weight(name)).then_inc(S["ld_small"], 16)
            sp.dma_start(router[:, :, :], dr["router"].rearrange("(c p) n -> p c n", p=P)).then_inc(S["ld_small"], 16)
            sp.dma_start(freqs[:, :], dr["freqs"][0:P, :]).then_inc(S["ld_small"], 16)
            with sp.Fori(1, BLOCKS, 1) as b:
                ctx_load(b, 0)
                ctx_load(b, 1)
            sp.wait_ge(S["pv_done"], BLOCKS * CHUNKS * GROUPS)
            sp.wait_ge(S["part_ready"], BLOCKS)
            for e in range(0, EXPERTS, 2):
                for big, name in ((w1, "w1"), (w3, "w3")):
                    for c in range(DC):
                        sp.dma_start(big[:, e:e + 2, c, :],
                                     dr[name][e:e + 2, c * P:(c + 1) * P, :].rearrange("e p n -> p e n")
                                     ).then_inc(S[f"ld_experts{e // 2}"], 16)
                for i in range(2):
                    sp.dma_start(w2[:, e + i, :, :], dr["w2"][e + i].rearrange("(c p) n -> p c n", p=P)
                                 ).then_inc(S[f"ld_experts{e // 2}"], 16)
            for m in range(EXPERTS // 2):
                sp.wait_ge(S[f"ld_experts{m}"], 16 * (2 * DC + 2))
                sp.sem_inc(S["experts_loaded"], 1)
            sp.wait_ge(S["dve_fin"], 1)
            sp.dma_start(out, fin[:, :]).then_inc(S["stored"], 16)
            sp.wait_ge(S["stored"], 16)

        @block.gpsimd
        def _(pool):
            pool.memset(ones[:, :], 1.0)
            pool.memset(val[:, :, :, HD:VW], 1.0)
            pool.memset(qparts[:, :, :].bitcast(F32), 0.0)
            pool.memset(maxparts[:, :].bitcast(F32), 0.0)
            for i in range(2):
                last = pool.memset(kparts[i][:, :, 96:P].bitcast(F32), 1.0)
            last.then_inc(S["pool_setup"], 1)
            pool.wait_ge(S["ld_q"], 16 * (1 + len(BIASES)))

            def context_low(b, j):
                n = b * CHUNKS + j
                pool.wait_ge(S["ch_ready"], n + 1)
                pool.tensor_tensor(cparts[j % 2][:, 1, :, :], ctxT[:, j % CHUNKS, :, :],
                                   cparts[j % 2][:, 0, :, :].bitcast(F32), ALU.subtract
                                   ).then_inc(S["cl_ready"], 1)

            def low_parts(n, i):
                pool.wait_ge(S["kh_ready"], n + 1)
                pool.tensor_tensor(
                    kparts[i][:, :, 32:64],
                    kvf[i][:, 0, :].rearrange("p (a c) -> p a c", c=32),
                    kparts[i][:, :, 0:32].bitcast(F32), ALU.subtract).then_inc(S["kl_ready"], 1)

            def values(b, j):
                if not isinstance(b, int) or b > 0:
                    pool.wait_ge(S["pv_done"], b * (CHUNKS * GROUPS) - (CHUNKS - j - 1) * GROUPS)
                pool.tensor_tensor(
                    val[:, j, :, 0:HD],
                    kvf[j % 2][:, 1, :].rearrange("p (h d) -> p h d", d=HD),
                    bv("bxv")[:, 0, :].rearrange("p (h d) -> p h d", d=HD), ALU.add).then_inc(S["val_ready"], 1)

            def steps(b, last):
                for s in range(STEPS):
                    values(b, 2 * s)
                    if not (last and s == STEPS - 1):
                        context_low(b, 2 * s + 2)
                        context_low(b, 2 * s + 3)
                    values(b, 2 * s + 1)
                    if not (last and s == STEPS - 1):
                        for j in (2 * s + 2, 2 * s + 3):
                            low_parts(b * CHUNKS + j, j % 2)

            context_low(0, 0)
            context_low(0, 1)
            low_parts(0, 0)
            low_parts(1, 1)
            steps(0, False)
            with pool.Fori(1, BLOCKS - 1, 1) as b:
                steps(b, False)
            steps(BLOCKS - 1, True)

        @block.scalar
        def _(act):
            def context_high(b, j):
                n = b * CHUNKS + j
                act.wait_ge(S[f"ld_ctx{j % CHUNKS // HALF}"], (b + j // CHUNKS) * 16 + 16)
                if not isinstance(b, int) or n >= 2:
                    act.wait_ge(S["kv_done"], n - 1)
                act.activation(cparts[j % 2][:, 0, :, :], ctxT[:, j % CHUNKS, :, :], ACT.Copy
                               ).then_inc(S["ch_ready"], 1)

            act.wait_ge(S["ld_kv"], 32)
            for i, name in enumerate(("xk", "xv")):
                last = act.activation(wkv[:, 0, :, i * D:(i + 1) * D], w[name][:, :, :], ACT.Copy)
            last.then_inc(S["act_wkvh"], 1)
            context_high(0, 0)
            context_high(0, 1)
            act.wait_ge(S["pe_qT"], GROUPS)
            for g in (1, 3):
                act.activation(qmat[0:96, GH * g:GH * (g + 1), :],
                               B[2 + g][0:96, :].rearrange("p (h q) -> p h q", q=P), ACT.Copy
                               ).then_inc(S["act_qmat"], 1)

            def high_parts(n, i):
                act.wait_ge(S["kvf_ready"], n + 1)
                if not isinstance(n, int) or n >= 2:
                    act.wait_ge(S["kt_done"], 2 * n - 2)
                for seg in (0, 2):
                    last = act.activation(kparts[i][:, :, 32 * seg:32 * seg + 32],
                                          kvf[i][:, 0, :].rearrange("p (a c) -> p a c", c=32), ACT.Copy)
                last.then_inc(S["kh_ready"], 1)

            def exponentials(c, j):
                for g in range(GROUPS):
                    n = c * (CHUNKS * GROUPS) + (GROUPS * j + g)
                    act.wait_ge(S["sc_done"], n + 1)
                    if j > 0:
                        act.wait_ge(S["pv_done"], n - (GROUPS - 1))
                    act.activation(probs[g][:, :, :],
                                   sc_bank[g][:, :].rearrange("p (h q) -> p h q", q=P), ACT.Exp
                                   ).then_inc(S["exp_ready"], 1)

            def steps(b, first, last):
                for s in range(STEPS):
                    if not first:
                        exponentials(b - 1, 2 * s)
                    if not (last and s == STEPS - 1):
                        context_high(b, 2 * s + 2)
                        context_high(b, 2 * s + 3)
                    if not first:
                        exponentials(b - 1, 2 * s + 1)
                    if not (last and s == STEPS - 1):
                        for j in (2 * s + 2, 2 * s + 3):
                            high_parts(b * CHUNKS + j, j % 2)

            act.wait_ge(S["pool_setup"], 1)
            high_parts(0, 0)
            high_parts(1, 1)
            steps(0, True, False)
            with act.Fori(1, BLOCKS - 1, 1) as b:
                steps(b, False, False)
            steps(BLOCKS - 1, False, True)
            for j in range(CHUNKS):
                exponentials(BLOCKS - 1, j)

            act.wait_ge(S["dve_dmax"], 1)
            act.activation(bmax[:, :, :], bmax[:, :, :], ACT.Exp).then_inc(S["act_bw"], 1)
            act.wait_ge(S["dve_a_neg"], 1)
            act.activation(tc[:, :], tc[:, :], ACT.Exp)
            act.activation(tb[:, D:2 * D], tb[:, D:2 * D], ACT.Exp, scale=-1.0).then_inc(S["act_a_exp"], 1)
            for g in range(GROUPS):
                act.wait_ge(S["dve_c_sub"], g + 1)
                act.activation(sm[:, GH * g:GH * (g + 1), :], sm[:, GH * g:GH * (g + 1), :], ACT.Exp,
                               scale=SCALE).then_inc(S["act_c_exp"], 1)
            for g in (1, 3):
                act.wait_ge(S["pe_c_pT"], g + 1)
                act.activation(pT[:, GH * g:GH * (g + 1), :],
                               B[g][:, :].rearrange("p (h q) -> p h q", q=P), ACT.Copy).then_inc(S["act_c_pT"], 1)
            act.wait_ge(S["dve_m_sub"], 1)
            act.activation(small[:, 8:16], small[:, 8:16], ACT.Exp).then_inc(S["act_m_exp"], 1)

            def expert(e, i):
                act.wait_ge(S["pe_m_h"], e + 1)
                if not isinstance(e, int) or e >= 2:
                    act.wait_ge(S["dve_m_g"], e - 1)
                act.activation(sig[i], B[i][:, :], ACT.Sigmoid).then_inc(S["act_m_sig"], 1)
                act.wait_ge(S["pe_m_gT"], e + 1)
                if not isinstance(e, int) or e >= 2:
                    act.wait_ge(S["pe_m_down"], e - 1)
                act.activation(gT[i], B[4 + i][:, :], ACT.Copy).then_inc(S["act_m_gT"], 1)

            sig = [sm[:, 4 * i:4 * i + 4, :].rearrange("p a b -> p (a b)") for i in range(2)]
            gT = [pT[:, 4 * i:4 * i + 4, :].rearrange("p a b -> p (a b)") for i in range(2)]
            for i in range(2):
                expert(i, i)
            with act.Fori(1, EXPERTS // 2, 1) as m:
                for i in range(2):
                    expert(m * 2 + i, i)

        @block.tensor
        def _(pe):
            def transpose_d(src, bank, done):
                for c in range(DC):
                    last = pe.transpose(bank[:, c * P:(c + 1) * P], src[:, c * P:(c + 1) * P], ident)
                last.then_inc(S[done], 1)

            def project(srcT, names, bank):
                for i, name in enumerate(names):
                    for c in range(DC):
                        last = pe.matmul(bank[:, i * D:(i + 1) * D], srcT[:, c, :], w[name][:, c, :],
                                         start=(c == 0), stop=(c == DC - 1))
                return last

            pe.wait_ge(S["ld_const"], 16)
            pe.wait_ge(S["dve_xn"], 1)
            transpose_d(xn, B[0], "pe_xnT")
            pe.wait_ge(S["dve_xnT"], 1)
            pe.wait_ge(S["ld_q"], 16 * (1 + len(BIASES)))
            project(xnT, ["xq"], B[1]).then_inc(S["pe_q"], 1)
            pe.wait_ge(S["dve_qparts"], 1)
            pe.wait_ge(S["dve_ident"], 1)
            pe.wait_ge(S["pool_setup"], 1)
            for g in range(GROUPS):
                for h in range(GH):
                    last = pe.transpose(B[2 + g][0:96, h * P:(h + 1) * P].bitcast(F32R), qparts[:, GH * g + h, :],
                                        ident_r[:, :])
                last.then_inc(S["pe_qT"], 1)

            def keys_values(b, j):
                n = b * CHUNKS + j
                pe.wait_ge(S["cl_ready"], n + 1)
                if not isinstance(b, int) or n >= 2:
                    pe.wait_ge(S["kvf_ready"], n - 1)
                products = [(a, v, c) for a, v in ((0, 0), (1, 0), (0, 1)) for c in range(DC)]
                for i, (a, v, c) in enumerate(products):
                    last = pe.matmul(kv_bank[j % 2][:, :], cparts[j % 2][:, a, c, :], wkv[:, v, c, :],
                                     start=(i == 0), stop=(i == len(products) - 1))
                last.then_inc(S["kv_done"], 1)

            def turn_keys(b, j, u, first=False):
                n = b * CHUNKS + j
                if u == 0:
                    pe.wait_ge(S["kl_ready"], n + 1)
                    if j == 0 and not first:
                        pe.wait_ge(S["qmat_ready"], b * GROUPS)
                if u == 1 or not isinstance(b, int) or n > 0:
                    pe.wait_ge(S["kt_ready"], 2 * n + u)
                for p in range(PAIRS // 2):
                    last = pe.transpose(kt_bank[:, p * P:(p + 1) * P].bitcast(F32R),
                                        kparts[j % 2][:, u * (PAIRS // 2) + p, :], ident_r[:, :])
                last.then_inc(S["kt_done"], 1)

            def max_scores(b, s, v, first):
                m = b * (8 * STEPS) + (8 * s + v)
                if v == 0:
                    pe.wait_ge(S["kt_ready"], b * (2 * CHUNKS) + 4 * (s + 1))
                if v >= 4 or (first and s > 0):
                    pe.wait_ge(S["mx_read"], m - 3)
                for a in range(2):
                    last = pe.matmul(sc_bank[v % 4][:, a * 2 * P:(a + 1) * 2 * P], qmat[0:96, 2 * v + a, :],
                                     kT[0:96, s, v, :], start=True, stop=True)
                last.then_inc(S["mx_done"], 1)

            def turn_max(b):
                pe.wait_ge(S["mparts_ready"], b * 2 + 2)
                pe.wait_ge(S["kt_ready"], b * (2 * CHUNKS) + 2 * CHUNKS)
                pe.transpose(kt_bank[:, 0:P].bitcast(F32R), maxparts[:, :], ident_r[:, :]).then_inc(S["mt_done"], 1)

            def scores(c, j, g, alone=False):
                n = c * (CHUNKS * GROUPS) + (GROUPS * j + g)
                if j == 0:
                    pe.wait_ge(S["qmat_ready"], c * GROUPS + (g + 1))
                elif j % 2 or alone:
                    pe.wait_ge(S["exp_ready"], n - 3)
                else:
                    pe.wait_ge(S["mx_read"], c * (8 * STEPS) + (8 * STEPS + 4 * j - 3 + g))
                for i in range(2):
                    p = 2 * g + i
                    last = pe.matmul(sc_bank[g][:, i * 2 * P:(i + 1) * 2 * P],
                                     kT[:, j // 2, p, (j % 2) * P:(j % 2 + 1) * P],
                                     qmat[:, 2 * p:2 * p + 2, :], start=True, stop=True)
                last.then_inc(S["sc_done"], 1)

            def weighted_values(c, j, g):
                n = c * (CHUNKS * GROUPS) + (GROUPS * j + g)
                pe.wait_ge(S["exp_ready"], n + 1)
                if g == 0:
                    pe.wait_ge(S["val_ready"], c * CHUNKS + (j + 1))
                for r in range(GH):
                    last = pe.matmul(pv_bank[32 * r:32 * r + VW, g * P:(g + 1) * P], val[:, j, GH * g + r, :],
                                     probs[g][:, r, :], start=(j == 0 and g == 0), stop=(j == CHUNKS - 1),
                                     skip_group_check=True)
                last.then_inc(S["pv_done"], 1)

            def steps(b, first, last):
                for s in range(STEPS):
                    if not first:
                        c, j = b - 1, 2 * s
                        for g in range(GROUPS):
                            scores(c, j, g)
                        turn_keys(b, j, 0)
                        weighted_values(c, j, 0)
                        weighted_values(c, j, 1)
                        scores(c, j + 1, 0)
                        scores(c, j + 1, 1)
                        turn_keys(b, j, 1)
                        weighted_values(c, j, 2)
                        weighted_values(c, j, 3)
                        scores(c, j + 1, 2)
                        scores(c, j + 1, 3)
                        turn_keys(b, j + 1, 0)
                        for g in range(GROUPS):
                            weighted_values(c, j + 1, g)
                        turn_keys(b, j + 1, 1)
                    else:
                        for j in (2 * s, 2 * s + 1):
                            for u in range(2):
                                turn_keys(b, j, u, True)
                    for v in range(8):
                        max_scores(b, s, v, first)
                        if v in (1, 5) and not (last and s == STEPS - 1):
                            keys_values(b, 2 * s + (2 if v == 1 else 3))
                turn_max(b)

            pe.wait_ge(S["dve_wkvl"], 2)
            pe.wait_ge(S["dve_pvzero"], 1)
            pe.wait_ge(S["dve_qmat"], 2)
            pe.wait_ge(S["act_qmat"], 2)
            keys_values(0, 0)
            keys_values(0, 1)
            steps(0, True, False)
            with pe.Fori(1, BLOCKS - 1, 1) as b:
                steps(b, False, False)
            steps(BLOCKS - 1, False, True)
            c = BLOCKS - 1
            for j in range(CHUNKS):
                for g in (0, 1):
                    scores(c, j, g, True)
                if j > 0:
                    weighted_values(c, j - 1, 2)
                    weighted_values(c, j - 1, 3)
                for g in (2, 3):
                    scores(c, j, g, True)
                weighted_values(c, j, 0)
                weighted_values(c, j, 1)
            weighted_values(c, CHUNKS - 1, 2)
            weighted_values(c, CHUNKS - 1, 3)

            pe.wait_ge(S["part_ready"], BLOCKS)
            for b in range(BLOCKS):
                if b >= 2:
                    pe.wait_ge(S["dve_partT_read"], b - 1)
                for g in range(GROUPS):
                    last = pe.transpose(B[5 + b % 2][:, g * P:(g + 1) * P], parts[:, b, g * P:(g + 1) * P], ident)
                last.then_inc(S["pe_partT"], 1)
            pe.wait_ge(S["dve_att"], 1)
            transpose_d(xn, B[0], "pe_attT")
            pe.wait_ge(S["dve_attT"], 1)
            pe.wait_ge(S["ld_small"], 16 * (len(WEIGHTS) - 3 + 2))
            project(xnT, ["xo"], B[1]).then_inc(S["pe_xo"], 1)

            pe.wait_ge(S["dve_a_xn"], 1)
            transpose_d(xn, B[0], "pe_a_xnT")
            pe.wait_ge(S["dve_a_xnT"], 1)
            project(xnT, ["aq", "ak"], B[1]).then_inc(S["pe_a_proj"], 1)
            project(xnT, ["av", "ag"], B[2]).then_inc(S["pe_a_proj"], 1)
            pe.wait_ge(S["dve_a_qkv"], 1)
            transpose_d(ta, B[3], "pe_a_qT")
            for c in range(DC):
                pe.matmul(B[4][:, c * D:c * D + P], ta[:, D + c * P:D + (c + 1) * P], tb[:, c * P:(c + 1) * P],
                          start=True, stop=True)
                last = pe.matmul(B[4][:, c * D + P:c * D + P + 1], ta[:, D + c * P:D + (c + 1) * P], ones[:, :],
                                 start=True, stop=True)
            last.then_inc(S["pe_a_kv"], 1)
            pe.wait_ge(S["dve_a_kvr"], 1)
            for c in range(DC):
                last = pe.matmul(B[5][:, c * D:c * D + P + H // DC], xnT[:, c, :], kvr[:, c, :], start=True, stop=True)
            last.then_inc(S["pe_a_num"], 1)
            pe.wait_ge(S["dve_a_out"], 1)
            transpose_d(xn, B[0], "pe_a_outT")
            pe.wait_ge(S["dve_a_outT"], 1)
            project(xnT, ["ao"], B[1]).then_inc(S["pe_a_o"], 1)

            pe.wait_ge(S["dve_c_xn"], 1)
            transpose_d(xn, B[0], "pe_c_xnT")
            pe.wait_ge(S["dve_c_xnT"], 1)
            project(xnT, ["fq", "fk"], B[1]).then_inc(S["pe_c_proj"], 1)
            project(xnT, ["fv"], B[2]).then_inc(S["pe_c_proj"], 1)
            pe.wait_ge(S["dve_c_qk"], 1)
            for c in range(2 * DC):
                last = pe.transpose(B[3][:, c * P:(c + 1) * P], ta[:, c * P:(c + 1) * P], ident)
            last.then_inc(S["pe_c_qkT"], 1)
            for c in range(DC):
                pe.wait_ge(S["dve_c_kbd"], c + 1)
                for u in range(2):
                    pe.matmul(B[4 + 2 * c + u][:, :], xnT[:, c, :], kbd[:, c, GH * u:GH * (u + 1), :],
                              start=True, stop=True).then_inc(S["pe_c_scores"], 1)
            for g in range(GROUPS):
                pe.wait_ge(S["act_c_exp"], g + 1)
                for h in range(GH):
                    last = pe.transpose(B[g][:, h * P:(h + 1) * P], sm[:, GH * g + h, :], ident)
                last.then_inc(S["pe_c_pT"], 1)
            pe.wait_ge(S["dve_c_pT"], 2)
            pe.wait_ge(S["act_c_pT"], 2)
            for g in range(GROUPS):
                for r in range(GH):
                    last = pe.matmul(B[4][32 * r:32 * r + VW, g * P:(g + 1) * P], vaug[:, GH * g + r, :],
                                     pT[:, GH * g + r, :], start=True, stop=True)
            last.then_inc(S["pe_c_pv"], 1)
            pe.wait_ge(S["dve_c_oT"], 1)
            for g in range(GROUPS):
                last = pe.transpose(B[5][:, g * P:(g + 1) * P], oT[:, g, :], ident)
            last.then_inc(S["pe_c_o"], 1)
            pe.wait_ge(S["dve_c_att"], 1)
            transpose_d(xn, B[0], "pe_c_attT")
            pe.wait_ge(S["dve_c_attT"], 1)
            project(xnT, ["fo"], B[1]).then_inc(S["pe_c_proj_o"], 1)

            pe.wait_ge(S["dve_m_t"], 1)
            transpose_d(xn, B[0], "pe_m_tT")
            pe.wait_ge(S["dve_m_tT"], 1)
            for c in range(DC):
                last = pe.matmul(B[7][:, 0:EXPERTS], xnT[:, c, :], router[:, c, :], start=(c == 0), stop=(c == DC - 1))
            last.then_inc(S["pe_m_logits"], 1)

            def up(m, i):
                e = m * 2 + i
                pe.wait_ge(S["experts_loaded"], m + 1)
                if not isinstance(e, int) or e >= 2:
                    pe.wait_ge(S["dve_m_g"], e - 1)
                for bank, big in ((B[i], w1), (B[2 + i], w3)):
                    for c in range(DC):
                        last = pe.matmul(bank[:, :], xnT[:, c, :], big[:, e, c, :], start=(c == 0), stop=(c == DC - 1))
                last.then_inc(S["pe_m_h"], 1)

            def turn(e, i):
                pe.wait_ge(S["dve_m_g"], e + 1)
                if not isinstance(e, int) or e >= 2:
                    pe.wait_ge(S["act_m_gT"], e - 1)
                for k in range(IC):
                    last = pe.transpose(B[4 + i][:, k * P:(k + 1) * P], sm[:, 8 + 4 * i + k, :], ident)
                last.then_inc(S["pe_m_gT"], 1)

            def down(e, i, first, final):
                pe.wait_ge(S["act_m_gT"], e + 1)

                for k in range(IC):
                    last = pe.matmul(B[6][:, 0:D], pT[:, 4 * i + k, :], w2[:, e, k, :],
                                     start=(first and k == 0), stop=(final and k == IC - 1))
                last.then_inc(S["pe_m_down"], 1)
                if final:
                    return last

            up(0, 0)
            up(0, 1)
            turn(0, 0)
            down(0, 0, True, False)
            with pe.Fori(1, EXPERTS // 2, 1) as m:
                up(m, 0)
                turn(m * 2 - 1, 1)
                down(m * 2 - 1, 1, False, False)
                up(m, 1)
                turn(m * 2, 0)
                down(m * 2, 0, False, False)
            turn(EXPERTS - 1, 1)
            down(EXPERTS - 1, 1, False, True)

        @block.vector
        def _(dve):
            links = [0]

            def link(ins):
                links[0] += 1
                ins.then_inc(S["dve_chain"], 1)
                dve.wait_ge(S["dve_chain"], links[0])

            def rsqrt(v, y, tmp):
                link(dve.tensor_scalar(tmp.bitcast(I32), v.bitcast(I32), 1, None, ALU.logical_shift_right))
                link(dve.tensor_scalar(y.bitcast(I32), tmp.bitcast(I32), -1.0, float(0x5F3759DF), ALU.mult, ALU.add))
                for _ in range(3):
                    link(dve.scalar_tensor_tensor(tmp, y, y, v, ALU.mult, ALU.mult))
                    link(dve.tensor_scalar(tmp, tmp, -0.5, 1.5, ALU.mult, ALU.add))
                    link(dve.tensor_tensor(y, y, tmp, ALU.mult))

            def layernorm(dst, src):
                link(dve.bn_stats(small[:, 0:6], src))
                link(dve.bn_aggr(small[:, 6:8], small[:, 0:6]))
                link(dve.tensor_scalar(small[:, 7:8], small[:, 7:8], EPS_LN, None, ALU.add))
                rsqrt(small[:, 7:8], small[:, 8:9], small[:, 9:10])
                return dve.tensor_scalar(dst, src, small[:, 6:7], small[:, 8:9], ALU.subtract, ALU.mult)

            def rmsnorm(dst, src, weight, tmp):
                link(dve.tensor_tensor(tmp, src, src, ALU.mult))
                link(dve.tensor_reduce(small[:, 0:1], tmp, AX_X, ALU.add))
                link(dve.tensor_scalar(small[:, 1:2], small[:, 0:1], 1.0 / D, EPS_RMS, ALU.mult, ALU.add))
                rsqrt(small[:, 1:2], small[:, 2:3], small[:, 3:4])
                return dve.scalar_tensor_tensor(dst, src, small[:, 2:3], weight, ALU.mult, ALU.mult)

            def turned(dst, bank, pe_signal, signal):
                dve.wait_ge(S[pe_signal], 1)
                dve.tensor_copy(dst[:, :, :], bank[:, 0:D].rearrange("p (c n) -> p c n", n=P)).then_inc(S[signal], 1)

            link(dve.memset(pv_bank[:, :], 0.0))
            dve.wait_ge(S["ld_x"], 16)
            layernorm(xn[:, :], x[:, :]).then_inc(S["dve_xn"], 1)
            dve.wait_ge(S["ld_const"], 16)
            dve.tensor_copy(ident_r[:, :], ident).then_inc(S["dve_ident"], 1)
            turned(xnT, B[0], "pe_xnT", "dve_xnT")
            dve.wait_ge(S["ld_q"], 16 * (1 + len(BIASES)))
            dve.memset(kbias[:, 1, :], 0.0)
            link(dve.tensor_copy(kbias[:, 0, :], bv("bxk")[:, 0, :]))
            dve.wait_ge(S["pe_q"], 1)
            q = kvf[0][:, 0, :]
            link(dve.tensor_tensor(q, B[1][:, 0:D], bv("bxq")[:, 0, :], ALU.add))
            dve.wait_ge(S["pool_setup"], 1)
            q4 = q.rearrange("p (m a d) -> p m a d", a=2, d=HD)
            qp4 = qparts[:, :, :].rearrange("p (m a) c -> p m a c", a=2)
            for seg in (0, 32):
                for a in range(2):
                    last = dve.tensor_scalar(qp4[:, :, a, seg + HD * a:seg + HD * (a + 1)], q4[:, :, a, :],
                                             SCALE, None, ALU.mult)
            link(last)
            for a in range(2):
                last = dve.scalar_tensor_tensor(qp4[:, :, a, 64 + HD * a:64 + HD * (a + 1)], q4[:, :, a, :], SCALE,
                                                qp4[:, :, a, HD * a:HD * (a + 1)].bitcast(F32), ALU.mult, ALU.subtract)
            last.then_inc(S["dve_qparts"], 1)
            for g in (0, 2):
                dve.wait_ge(S["pe_qT"], g + 1)
                dve.tensor_copy(qmat[0:96, GH * g:GH * (g + 1), :],
                                B[2 + g][0:96, :].rearrange("p (h q) -> p h q", q=P)).then_inc(S["dve_qmat"], 1)
            dve.wait_ge(S["act_qmat"], 2)
            dve.memset(pv_bank[:, :], 0.0).then_inc(S["dve_pvzero"], 1)

            dve.wait_ge(S["act_wkvh"], 1)
            for i, name in enumerate(("xk", "xv")):
                dve.tensor_tensor(wkv[:, 1, :, i * D:(i + 1) * D], w[name][:, :, :],
                                  wkv[:, 0, :, i * D:(i + 1) * D].bitcast(F32), ALU.subtract
                                  ).then_inc(S["dve_wkvl"], 1)

            def kv_out(n, i):
                dve.wait_ge(S["kv_done"], n + 1)
                if not isinstance(n, int) or n >= 2:
                    dve.wait_ge(S["val_ready"], n - 1)
                    dve.wait_ge(S["kl_ready"], n - 1)
                dve.tensor_tensor(kvf[i][:, :, :], kv_bank[i][:, :].rearrange("p (s n) -> p s n", s=2),
                                  kbias[:, :, :], ALU.add).then_inc(S["kvf_ready"], 1)

            def keys_out(b, j):
                for u in range(2):
                    dve.wait_ge(S["kt_done"], b * (2 * CHUNKS) + (2 * j + u + 1))
                    dve.tensor_copy(kT[:, j // 2, 4 * u:4 * u + 4, (j % 2) * P:(j % 2 + 1) * P],
                                    kt_bank[:, :].rearrange("p (a k) -> p a k", k=P)).then_inc(S["kt_ready"], 1)

            def step_max(b, s, v):
                dve.wait_ge(S["mx_done"], b * (8 * STEPS) + (8 * s + v + 1))
                dve.tensor_reduce(stepmax[:, s, 2 * v:2 * v + 2],
                                  sc_bank[v % 4][:, :].rearrange("p (a k) -> p a k", a=2), AX_X, ALU.max
                                  ).then_inc(S["mx_read"], 1)

            def block_max(b):
                dve.wait_ge(S["mx_read"], b * (8 * STEPS) + 8 * STEPS)
                dve.tensor_reduce(curmax[:, :], stepmax[:, :, :].rearrange("p s h -> p h s"), AX_X, ALU.max
                                  ).then_inc(S["curmax_ready"], 1)
                dve.wait_ge(S["curmax_ready"], b + 1)
                dve.tensor_scalar(maxparts[:, 96:96 + H], curmax[:, :], -1.0, None, ALU.mult
                                  ).then_inc(S["mparts_ready"], 1)
                dve.wait_ge(S["mparts_ready"], b * 2 + 1)
                dve.scalar_tensor_tensor(maxparts[:, 96 + H:P], curmax[:, :], -1.0,
                                         maxparts[:, 96:96 + H].bitcast(F32), ALU.mult, ALU.subtract
                                         ).then_inc(S["mparts_ready"], 1)
                dve.tensor_scalar(bmax[:, b, :], curmax[:, :], 1.0, None, ALU.mult).then_inc(S["bmax_ready"], 1)
                dve.wait_ge(S["mt_done"], b + 1)
                for g in range(GROUPS):
                    dve.tensor_tensor(qmat[96:P, GH * g:GH * (g + 1), :],
                                      over_heads(kt_bank[96:P, 0:P], GH),
                                      per_head(const[96:P, C_MM + GH * g:C_MM + GH * (g + 1)], P), ALU.mult
                                      ).then_inc(S["qmat_ready"], 1)

            def part_out(c):
                dve.wait_ge(S["pv_done"], c * (CHUNKS * GROUPS) + CHUNKS * GROUPS)
                dve.tensor_scalar(parts[:, c, :], pv_bank[:, :], 1.0, None, ALU.mult).then_inc(S["part_ready"], 1)

            def steps(b, first, last):
                for s in range(STEPS):
                    keys_out(b, 2 * s)
                    keys_out(b, 2 * s + 1)
                    if s == STEPS - 1 and not first:
                        part_out(b - 1)
                    for v in range(8):
                        step_max(b, s, v)
                        if v in (2, 6) and not (last and s == STEPS - 1):
                            j = 2 * s + (2 if v == 2 else 3)
                            kv_out(b * CHUNKS + j, j % 2)
                block_max(b)

            kv_out(0, 0)
            kv_out(1, 1)
            steps(0, True, False)
            with dve.Fori(1, BLOCKS - 1, 1) as b:
                steps(b, False, False)
            steps(BLOCKS - 1, False, True)
            part_out(BLOCKS - 1)

            dve.wait_ge(S["bmax_ready"], BLOCKS)
            link(dve.tensor_reduce(small[:, 16:32], bmax[:, :, :].rearrange("p b h -> p h b"), AX_X, ALU.max))
            dve.tensor_tensor(bmax[:, :, :], bmax[:, :, :], over_heads(small[:, 16:32], BLOCKS), ALU.subtract
                              ).then_inc(S["dve_dmax"], 1)
            dve.wait_ge(S["act_bw"], 1)
            merged = ta[:, 0:H * VW].rearrange("p (h v) -> p h v", v=VW)
            piece = tb[:, 0:H * VW].rearrange("p (h v) -> p h v", v=VW)
            for b in range(BLOCKS):
                dve.wait_ge(S["pe_partT"], b + 1)
                bank = B[5 + b % 2][:, :].rearrange("p (h v) -> p h v", v=32)[:, :, 0:VW]
                ins = dve.tensor_tensor(merged if b == 0 else piece, bank, per_head(bmax[:, b, :], VW), ALU.mult)
                ins.then_inc(S["dve_partT_read"], 1)
                dve.wait_ge(S["dve_partT_read"], b + 1)
                if b:
                    link(dve.tensor_tensor(merged, merged, piece, ALU.add))
            link(dve.reciprocal(small[:, 32:48], merged[:, :, HD]))
            dve.tensor_tensor(xn[:, :].rearrange("p (h d) -> p h d", d=HD), merged[:, :, 0:HD],
                              per_head(small[:, 32:48], HD), ALU.mult).then_inc(S["dve_att"], 1)
            turned(xnT, B[0], "pe_attT", "dve_attT")
            dve.wait_ge(S["pe_xo"], 1)
            link(dve.tensor_tensor(x1[:, :], B[1][:, 0:D], bv("bxo")[:, 0, :], ALU.add))
            link(dve.tensor_tensor(x1[:, :], x1[:, :], x[:, :], ALU.add))

            layernorm(xn[:, :], x1[:, :]).then_inc(S["dve_a_xn"], 1)
            turned(xnT, B[0], "pe_a_xnT", "dve_a_xnT")
            dve.wait_ge(S["pe_a_proj"], 1)
            link(dve.tensor_tensor(ta[:, :].rearrange("p (s n) -> p s n", s=2),
                                   B[1][:, :].rearrange("p (s n) -> p s n", s=2), bv("baq", 2), ALU.add))
            dve.tensor_scalar(tc[:, :], ta[:, :], 0.0, None, ALU.min)
            dve.wait_ge(S["pe_a_proj"], 2)
            dve.tensor_tensor(tb[:, :].rearrange("p (s n) -> p s n", s=2),
                              B[2][:, :].rearrange("p (s n) -> p s n", s=2), bv("bav", 2), ALU.add
                              ).then_inc(S["dve_a_neg"], 1)
            dve.wait_ge(S["act_a_exp"], 1)
            dve.scalar_tensor_tensor(ta[:, :], ta[:, :], 0.0, tc[:, :], ALU.max, ALU.add).then_inc(S["dve_a_qkv"], 1)
            link(dve.tensor_scalar(tb[:, D:2 * D], tb[:, D:2 * D], 1.0, None, ALU.add))
            dve.reciprocal(tc[:, 0:D], tb[:, D:2 * D])
            dve.wait_ge(S["pe_a_qT"], 1)
            dve.tensor_copy(xnT[:, :, :], B[3][:, 0:D].rearrange("p (c n) -> p c n", n=P))
            dve.wait_ge(S["pe_a_kv"], 1)
            for c in range(DC):
                dve.tensor_tensor(kvr[:, c, 0:P], B[4][:, c * D:c * D + P], const[:, C_BM:C_BM + P], ALU.mult)
                last = dve.tensor_scalar(kvr[:, c, P:P + H // DC], const[:, C_HM:C_HM + H // DC],
                                         B[4][:, c * D + P:c * D + P + 1], None, ALU.mult)
            last.then_inc(S["dve_a_kvr"], 1)
            dve.wait_ge(S["pe_a_num"], 1)
            num = B[5][:, :].rearrange("p (c n) -> p c n", c=DC)
            zz = small[:, 16:32].rearrange("p (c h) -> p c h", c=DC)
            link(dve.tensor_scalar(zz, num[:, :, P:P + H // DC], EPS_Z, None, ALU.add))
            link(dve.reciprocal(small[:, 32:48], small[:, 16:32]))
            for c in range(DC):
                last = dve.tensor_tensor(ta[:, c * P:(c + 1) * P].rearrange("p (h d) -> p h d", d=HD),
                                         num[:, c, 0:P].rearrange("p (h d) -> p h d", d=HD),
                                         per_head(small[:, 32 + 8 * c:40 + 8 * c], HD), ALU.mult)
            link(last)
            dve.tensor_tensor(xn[:, :], ta[:, 0:D], tc[:, 0:D], ALU.mult).then_inc(S["dve_a_out"], 1)
            turned(xnT, B[0], "pe_a_outT", "dve_a_outT")
            dve.wait_ge(S["pe_a_o"], 1)
            link(dve.tensor_tensor(x2[:, :], B[1][:, 0:D], bv("bao")[:, 0, :], ALU.add))
            link(dve.tensor_tensor(x2[:, :], x2[:, :], x1[:, :], ALU.add))

            link(layernorm(xl[:, :], x2[:, :]))
            rmsnorm(xn[:, :], xl[:, :], bv("anw")[:, 0, :], tb[:, 0:D]).then_inc(S["dve_c_xn"], 1)
            turned(xnT, B[0], "pe_c_xnT", "dve_c_xnT")
            dve.memset(vaug[:, :, HD:VW], 1.0)
            dve.wait_ge(S["pe_c_proj"], 1)
            pairs = B[1][:, :].rearrange("p (h j e) -> p h j e", h=2 * H, e=2)
            turnedqk = ta[:, :].rearrange("p (h j e) -> p h j e", h=2 * H, e=2)
            fr = freqs[:, :].rearrange("p (j e) -> p j e", e=2)
            cos, sin = (over_heads(fr[:, :, e], 2 * H) for e in range(2))
            t0, t1, t2, t3 = (v.rearrange("p (h j) -> p h j", j=HD // 2)
                              for v in (tb[:, 0:D], tb[:, D:2 * D], tc[:, 0:D], tc[:, D:2 * D]))
            dve.tensor_tensor(t0, pairs[:, :, :, 0], cos, ALU.mult)
            dve.tensor_tensor(t1, pairs[:, :, :, 1], sin, ALU.mult)
            dve.tensor_tensor(t2, pairs[:, :, :, 0], sin, ALU.mult)
            link(dve.tensor_tensor(t3, pairs[:, :, :, 1], cos, ALU.mult))
            dve.tensor_tensor(turnedqk[:, :, :, 0], t0, t1, ALU.subtract)
            dve.tensor_tensor(turnedqk[:, :, :, 1], t2, t3, ALU.add).then_inc(S["dve_c_qk"], 1)
            dve.wait_ge(S["pe_c_proj"], 2)
            dve.tensor_copy(vaug[:, :, 0:HD], B[2][:, 0:D].rearrange("p (h d) -> p h d", d=HD))
            dve.wait_ge(S["pe_c_qkT"], 1)
            dve.tensor_copy(xnT[:, :, :], B[3][:, 0:D].rearrange("p (c n) -> p c n", n=P))
            for c in range(DC):
                dve.tensor_tensor(kbd[:, c, :, :], over_heads(B[3][:, D + c * P:D + (c + 1) * P], H // DC),
                                  per_head(const[:, C_HM:C_HM + H // DC], P), ALU.mult).then_inc(S["dve_c_kbd"], 1)
            for g in range(GROUPS):
                s4 = sm[:, GH * g:GH * (g + 1), :]
                dve.wait_ge(S["pe_c_scores"], g + 1)
                link(dve.tensor_tensor(s4, B[4 + g][:, :].rearrange("p (h k) -> p h k", k=P),
                                       over_heads(const[:, C_CA:C_CA + P], GH), ALU.add))
                link(dve.tensor_reduce(small[:, 16 + GH * g:16 + GH * (g + 1)], s4, AX_X, ALU.max))
                dve.tensor_tensor(s4, s4, per_head(small[:, 16 + GH * g:16 + GH * (g + 1)], P), ALU.subtract
                                  ).then_inc(S["dve_c_sub"], 1)
            for g in (0, 2):
                dve.wait_ge(S["pe_c_pT"], g + 1)
                dve.tensor_copy(pT[:, GH * g:GH * (g + 1), :],
                                B[g][:, :].rearrange("p (h q) -> p h q", q=P)).then_inc(S["dve_c_pT"], 1)
            dve.wait_ge(S["pe_c_pv"], 1)
            dve.tensor_copy(oT[:, :, :], B[4][:, :].rearrange("p (g q) -> p g q", q=P)).then_inc(S["dve_c_oT"], 1)
            dve.wait_ge(S["pe_c_o"], 1)
            o = B[5][:, :].rearrange("p (h v) -> p h v", v=32)
            link(dve.reciprocal(small[:, 32:48], o[:, :, HD]))
            dve.tensor_tensor(xn[:, :].rearrange("p (h d) -> p h d", d=HD), o[:, :, 0:HD],
                              per_head(small[:, 32:48], HD), ALU.mult).then_inc(S["dve_c_att"], 1)
            turned(xnT, B[0], "pe_c_attT", "dve_c_attT")
            dve.wait_ge(S["pe_c_proj_o"], 1)
            link(dve.tensor_tensor(hres[:, :], B[1][:, 0:D], xl[:, :], ALU.add))

            rmsnorm(xn[:, :], hres[:, :], bv("fnw")[:, 0, :], tb[:, 0:D]).then_inc(S["dve_m_t"], 1)
            turned(xnT, B[0], "pe_m_tT", "dve_m_tT")
            link(dve.tensor_tensor(hres[:, :], hres[:, :], x2[:, :], ALU.add))
            dve.wait_ge(S["pe_m_logits"], 1)
            E = EXPERTS
            link(dve.tensor_reduce(small[:, 0:1], B[7][:, 0:E], AX_X, ALU.max))
            dve.tensor_scalar(small[:, 8:16], B[7][:, 0:E], small[:, 0:1], None, ALU.subtract
                              ).then_inc(S["dve_m_sub"], 1)
            dve.wait_ge(S["act_m_exp"], 1)
            pr = small[:, 16:24]
            link(dve.tensor_reduce(small[:, 1:2], small[:, 8:16], AX_X, ALU.add))
            link(dve.reciprocal(small[:, 2:3], small[:, 1:2]))
            link(dve.tensor_scalar(pr, small[:, 8:16], small[:, 2:3], None, ALU.mult))
            big = small[:, 64:128].rearrange("p (a b) -> p a b", b=E)
            same = small[:, 128:192].rearrange("p (a b) -> p a b", b=E)
            dve.tensor_tensor(big, over_heads(pr, E), per_head(pr, E), ALU.is_gt)
            link(dve.tensor_tensor(same, over_heads(pr, E), per_head(pr, E), ALU.is_equal))
            link(dve.tensor_tensor(same, same, const[:, C_LT:C_LT + E * E].rearrange("p (a b) -> p a b", b=E),
                                   ALU.mult))
            link(dve.tensor_tensor(big, big, same, ALU.add))
            link(dve.tensor_reduce(small[:, 24:32], big, AX_X, ALU.add))
            link(dve.scalar_tensor_tensor(small[:, 32:40], small[:, 24:32], 1.5, pr, ALU.is_lt, ALU.mult))
            link(dve.tensor_reduce(small[:, 3:4], small[:, 32:40], AX_X, ALU.add))
            link(dve.reciprocal(small[:, 4:5], small[:, 3:4]))
            link(dve.tensor_scalar(share[:, :, 0], small[:, 32:40], small[:, 4:5], None, ALU.mult))

            def gated(e, i):
                sig = sm[:, 4 * i:4 * i + 4, :].rearrange("p a b -> p (a b)")
                g = sm[:, 8 + 4 * i:12 + 4 * i, :].rearrange("p a b -> p (a b)")
                dve.wait_ge(S["act_m_sig"], e + 1)
                if not isinstance(e, int) or e >= 2:
                    dve.wait_ge(S["pe_m_gT"], e - 1)
                dve.tensor_tensor(sig, sig, B[i][:, :], ALU.mult).then_inc(S["dve_m_w"], 1)
                dve.wait_ge(S["dve_m_w"], e + 1)
                dve.scalar_tensor_tensor(g, sig, share[:, e, :], B[2 + i][:, :], ALU.mult, ALU.mult
                                         ).then_inc(S["dve_m_g"], 1)

            gated(0, 0)
            gated(1, 1)
            with dve.Fori(1, EXPERTS // 2, 1) as m:
                gated(m * 2, 0)
                gated(m * 2 + 1, 1)
            dve.wait_ge(S["pe_m_down"], EXPERTS)
            dve.tensor_tensor(fin[:, :], B[6][:, 0:D], hres[:, :], ALU.add).then_inc(S["dve_fin"], 1)


MATRICES = {"w_xq": ("L0_xattn_Wq", True), "w_xk": ("L0_xattn_Wk", True), "w_xv": ("L0_xattn_Wv", True),
            "w_xo": ("L0_xattn_Wo", True), "w_aq": ("L0_attn_wq_w", False), "w_ak": ("L0_attn_wk_w", False),
            "w_av": ("L0_attn_wv_w", False), "w_ag": ("L0_attn_wg_w", False), "w_ao": ("L0_attn_out_w", False),
            "w_fq": ("L0_ffn_wq", False), "w_fk": ("L0_ffn_wk", False), "w_fv": ("L0_ffn_wv", False),
            "w_fo": ("L0_ffn_wo", False), "router": ("L0_ffn_router_w", False), "freqs": ("L0_ffn_freqs_cis", False),
            "w1": ("L0_ffn_w1", False), "w3": ("L0_ffn_w3", False), "w2": ("L0_ffn_w2", False)}
VECTORS = {"bxq": "L0_xattn_bq", "bxk": "L0_xattn_bk", "bxv": "L0_xattn_bv", "bxo": "L0_xattn_bo",
           "baq": "L0_attn_wq_b", "bak": "L0_attn_wk_b", "bav": "L0_attn_wv_b", "bag": "L0_attn_wg_b",
           "bao": "L0_attn_out_b", "anw": "L0_ffn_attn_norm_w", "fnw": "L0_ffn_ffn_norm_w"}


def constants(np):
    c = np.zeros((P, C_N), np.float32)
    i = np.arange(P)
    c[:, C_ID:C_ID + P] = np.eye(P)
    c[:, C_BM:C_BM + P] = i[:, None] // HD == i[None, :] // HD
    c[:, C_CA:C_CA + P] = np.where(i[:, None] >= i[None, :], 0.0, MASKED)
    c[:, C_HM:C_HM + P // HD] = i[:, None] // HD == np.arange(P // HD)[None, :]
    c[96:, C_MM:C_MM + H] = np.arange(32)[:, None] % H == np.arange(H)[None, :]
    e = np.arange(EXPERTS)
    c[:, C_LT:] = (e[None, :] < e[:, None]).reshape(1, -1)
    return c


def kernel(**inputs):
    import numpy as np
    import concourse.bacc as bacc
    from concourse.bass_utils import run_bass_kernel_spmd

    nc = bacc.Bacc("TRN2", target_bir_lowering=False, num_devices=1)
    arrays = {"x": np.asarray(inputs["x"]).reshape(P, D), "const": constants(np)}
    c = np.asarray(inputs["ctx_1024"]).reshape(BLOCKS, 2, HALF, P, DC, P)
    arrays["ctxT"] = c.transpose(0, 1, 5, 2, 4, 3).reshape(BLOCKS, 2, P, HALF * DC * P)
    for name, (given, turned) in MATRICES.items():
        a = np.asarray(inputs[given])
        arrays[name] = a.T if turned else a
    for name, given in VECTORS.items():
        arrays[name] = np.asarray(inputs[given])
    arrays = {n: np.ascontiguousarray(a) for n, a in arrays.items()}
    dr = {n: nc.dram_tensor(f"in_{n}", a.shape, mybir.dt.from_np(a.dtype), kind="ExternalInput").ap()
          for n, a in arrays.items()}
    out = nc.dram_tensor("out", (P, D), F32, kind="ExternalOutput").ap()
    perceiver_layer(nc, dr, out)
    r = run_bass_kernel_spmd(nc, [{f"in_{n}": a for n, a in arrays.items()}], core_ids=[0])
    return r.results[0]["out"].reshape(1, P, D)
```

```python
from contextlib import ExitStack

import concourse.bass as bass
from concourse import mybir

F32 = mybir.dt.float32
F32R = mybir.dt.float32r
I32 = mybir.dt.int32
ALU = mybir.AluOpType
ACT = mybir.ActivationFunctionType
AX_X = mybir.AxisListType.X

P = 128
D = 256
DC = D // P
H = 16
HD = D // H
VW = HD + 1
PAIRS = H // 2
KEYS = 12544
BLOCKS = 7
CHUNKS = KEYS // P // BLOCKS
STEPS = CHUNKS // 2
HALF = CHUNKS // 2
GROUPS = 4
GH = H // GROUPS
EXPERTS = 8
INNER = 512
IC = INNER // P
SCALE = 0.25
MASKED = -4.0e9
EPS_LN, EPS_RMS, EPS_Z = 1e-5, 1e-6, 1e-6

WEIGHTS = ["xq", "xk", "xv", "xo", "aq", "ak", "av", "ag", "ao", "fq", "fk", "fv", "fo"]
BIASES = ["bxq", "bxk", "bxv", "bxo", "baq", "bak", "bav", "bag", "bao", "anw", "fnw"]
C_ID, C_BM, C_CA, C_HM, C_MM, C_LT = 0, 128, 256, 384, 392, 408
C_N = C_LT + EXPERTS * EXPERTS

COUNTING = [
    "ch_ready",
    "cl_ready",
    "kv_done",
    "kvf_ready",
    "kh_ready",
    "kl_ready",
    "val_ready",
    "kt_done",
    "kt_ready",
    "mx_done",
    "mx_read",
    "curmax_ready",
    "mparts_ready",
    "mt_done",
    "qmat_ready",
    "bmax_ready",
    "sc_done",
    "exp_ready",
    "pv_done",
    "part_ready",
]
ONCE = [
    "pool_setup", "dve_ident", "dve_pvzero", "act_wkvh", "dve_wkvl",
    "dve_xn", "pe_xnT", "dve_xnT", "pe_q", "dve_qparts", "pe_qT", "dve_qmat", "act_qmat",
    "dve_dmax", "act_bw", "pe_partT", "dve_partT_read",
    "dve_att", "pe_attT", "dve_attT", "pe_xo",
    "dve_a_xn", "pe_a_xnT", "dve_a_xnT", "pe_a_proj", "dve_a_neg", "act_a_exp", "dve_a_qkv",
    "pe_a_qT", "pe_a_kv", "dve_a_kvr", "pe_a_num", "dve_a_out", "pe_a_outT", "dve_a_outT", "pe_a_o",
    "dve_c_xn", "pe_c_xnT", "dve_c_xnT", "pe_c_proj", "dve_c_qk", "pe_c_qkT", "dve_c_kbd",
    "pe_c_scores", "dve_c_sub", "act_c_exp", "pe_c_pT", "dve_c_pT", "act_c_pT", "pe_c_pv",
    "dve_c_oT", "pe_c_o", "dve_c_att", "pe_c_attT", "dve_c_attT", "pe_c_proj_o",
    "dve_m_t", "pe_m_tT", "dve_m_tT", "pe_m_logits", "dve_m_sub", "act_m_exp", "dve_m_w",
    "pe_m_h", "act_m_sig", "dve_m_g", "pe_m_gT", "act_m_gT", "pe_m_down", "pe_m_all",
    "dve_fin",
]
LOADS = ["ld_x", "ld_const", "ld_q", "ld_kv", "ld_ctx0", "ld_ctx1", "ld_small", "ld_experts0",
         "ld_experts1", "ld_experts2", "ld_experts3", "experts_loaded", "stored"]


def perceiver_layer(nc, dr, out):
    ctx = ExitStack()
    with ctx:
        def sb(name, shape, dt=F32):
            return ctx.enter_context(nc.sbuf_tensor(name, shape, dt))

        S = {n: ctx.enter_context(nc.semaphore(n)) for n in COUNTING + ONCE + LOADS + ["dve_chain"]}

        x = sb("x_in", [P, D])
        w = {n: sb("w_" + n, [P, DC, D]) for n in WEIGHTS}
        router = sb("router", [P, DC, EXPERTS])
        bias = sb("bias", [P, len(BIASES), D])
        const = sb("const", [P, C_N])
        freqs = sb("freqs", [P, HD])
        ident_r = sb("ident_r", [P, P], F32R)
        ones = sb("ones", [P, 1])
        parts = sb("parts", [P, BLOCKS, GROUPS * P])
        bmax = sb("bmax", [P, BLOCKS, H])
        small = sb("small", [P, 512])
        xn = sb("xn", [P, D])
        xnT = sb("xnT", [P, DC, P])

        ARENA = 142 * 1024
        at = [(nc.sbuf_base + 31) // 32 * 32]
        arena_end = at[0] + ARENA
        sb("arena", [P, ARENA // 4])
        arena_start = at[0]

        def place(name, shape, dt=F32):
            size = 4
            for n in shape[1:]:
                size *= n
            h = nc.alloc_sbuf_tensor_at(name, shape, dt, offset=at[0])
            at[0] += (size + 31) // 32 * 32
            assert at[0] <= arena_end, (name, at[0] - arena_end)
            return h

        kT = place("kT", [P, STEPS, PAIRS, 2 * P], F32R)
        ctxT = place("ctxT", [P, CHUNKS, DC, P])
        kparts = [place(f"kparts{i}", [P, PAIRS, P], F32R) for i in range(2)]
        val = place("val", [P, CHUNKS, H, VW])
        cparts = [place(f"cparts{i}", [P, 2, DC, P], F32R) for i in range(2)]
        wkv = place("wkv", [P, 2, DC, 2 * D], F32R)
        kvf = [place(f"kvf{i}", [P, 2, D]) for i in range(2)]
        kbias = place("kbias", [P, 2, D])
        probs = [place(f"probs{i}", [P, GH, P]) for i in range(GROUPS)]
        qmat = place("qmat", [P, H, P], F32R)
        qparts = place("qparts", [P, H, 96], F32R)
        stepmax = place("stepmax", [P, STEPS, H])
        curmax = place("curmax", [P, H])
        maxparts = place("maxparts", [P, P], F32R)

        at[0] = arena_start
        w3 = place("w3", [P, EXPERTS, DC, INNER])
        w1 = place("w1", [P, EXPERTS, DC, INNER])
        w2 = place("w2", [P, EXPERTS, IC, D])
        ta = place("ta", [P, 2 * D])
        tb = place("tb", [P, 2 * D])
        tc = place("tc", [P, 2 * D])
        sm = place("sm", [P, H, P])
        pT = place("pT", [P, H, P])
        kbd = place("kbd", [P, DC, H // DC, P])
        oT = place("oT", [P, GROUPS, P])
        vaug = place("vaug", [P, H, VW])
        kvr = place("kvr", [P, DC, P + H // DC])
        x1, x2, xl, hres = (place(n, [P, D]) for n in ("x1", "x2", "xl", "hres"))
        fin = place("fin", [P, D])
        share = place("share", [P, EXPERTS, 1])

        B = [ctx.enter_context(nc.psum_tensor(f"bank{i}", [P, 512], F32)) for i in range(8)]
        kv_bank, kt_bank, mx_bank, sc_bank, pv_bank = B[0], B[1], B[2:4], B[4:7], B[7]

        ident = const[:, C_ID:C_ID + P]

        def bv(first, n=1):
            i = BIASES.index(first)
            return bias[:, i:i + n, :]

        def per_head(v, n):
            return v.unsqueeze(2).broadcast_to([v.shape[0], v.shape[1], n])

        def over_heads(v, n):
            return v.unsqueeze(1).broadcast_to([v.shape[0], n, v.shape[1]])

        block = ctx.enter_context(nc.Block())

        @block.sync
        def _(sp):
            def ctx_load(b, half):
                if not isinstance(b, int) or b > 0:
                    sp.wait_ge(S["cl_ready"], b * CHUNKS - CHUNKS + HALF * (half + 1))
                sp.dma_start(ctxT[:, HALF * half:HALF * (half + 1), :, :],
                             dr["ctxT"][b, half]).then_inc(S[f"ld_ctx{half}"], 16)

            def weight(name):
                return w[name][:, :, :], dr["w_" + name].rearrange("(c p) n -> p c n", p=P)

            sp.dma_start(x[:, :], dr["x"]).then_inc(S["ld_x"], 16)
            sp.dma_start(const[:, :], dr["const"]).then_inc(S["ld_const"], 16)
            sp.dma_start(*weight("xq")).then_inc(S["ld_q"], 16)
            for n, name in enumerate(BIASES):
                sp.dma_start(bias[:, n, :], dr[name].partition_broadcast(P)).then_inc(S["ld_q"], 16)
            sp.dma_start(*weight("xk")).then_inc(S["ld_kv"], 16)
            sp.dma_start(*weight("xv")).then_inc(S["ld_kv"], 16)
            ctx_load(0, 0)
            ctx_load(0, 1)
            for name in WEIGHTS[3:]:
                sp.dma_start(*weight(name)).then_inc(S["ld_small"], 16)
            sp.dma_start(router[:, :, :], dr["router"].rearrange("(c p) n -> p c n", p=P)).then_inc(S["ld_small"], 16)
            sp.dma_start(freqs[:, :], dr["freqs"][0:P, :]).then_inc(S["ld_small"], 16)
            with sp.Fori(1, BLOCKS, 1) as b:
                ctx_load(b, 0)
                ctx_load(b, 1)
            sp.wait_ge(S["pv_done"], BLOCKS * CHUNKS * GROUPS)
            sp.wait_ge(S["part_ready"], BLOCKS)
            for e in range(0, EXPERTS, 2):
                for big, name in ((w1, "w1"), (w3, "w3")):
                    for c in range(DC):
                        sp.dma_start(big[:, e:e + 2, c, :],
                                     dr[name][e:e + 2, c * P:(c + 1) * P, :].rearrange("e p n -> p e n")
                                     ).then_inc(S[f"ld_experts{e // 2}"], 16)
                for i in range(2):
                    sp.dma_start(w2[:, e + i, :, :], dr["w2"][e + i].rearrange("(c p) n -> p c n", p=P)
                                 ).then_inc(S[f"ld_experts{e // 2}"], 16)
            for m in range(EXPERTS // 2):
                sp.wait_ge(S[f"ld_experts{m}"], 16 * (2 * DC + 2))
                sp.sem_inc(S["experts_loaded"], 1)
            sp.wait_ge(S["dve_fin"], 1)
            sp.dma_start(out, fin[:, :]).then_inc(S["stored"], 16)
            sp.wait_ge(S["stored"], 16)

        @block.gpsimd
        def _(pool):
            pool.memset(ones[:, :], 1.0)
            pool.memset(val[:, :, :, HD:VW], 1.0)
            pool.memset(qparts[:, :, :].bitcast(F32), 0.0)
            pool.memset(maxparts[:, :].bitcast(F32), 0.0)
            for i in range(2):
                last = pool.memset(kparts[i][:, :, 96:P].bitcast(F32), 1.0)
            last.then_inc(S["pool_setup"], 1)
            pool.wait_ge(S["ld_q"], 16 * (1 + len(BIASES)))

            def context_low(b, j):
                n = b * CHUNKS + j
                pool.wait_ge(S["ch_ready"], n + 1)
                pool.tensor_tensor(cparts[j % 2][:, 1, :, :], ctxT[:, j % CHUNKS, :, :],
                                   cparts[j % 2][:, 0, :, :].bitcast(F32), ALU.subtract
                                   ).then_inc(S["cl_ready"], 1)

            def low_parts(n, i):
                pool.wait_ge(S["kh_ready"], n + 1)
                pool.tensor_tensor(
                    kparts[i][:, :, 32:64],
                    kvf[i][:, 0, :].rearrange("p (a c) -> p a c", c=32),
                    kparts[i][:, :, 0:32].bitcast(F32), ALU.subtract).then_inc(S["kl_ready"], 1)

            def values(b, j):
                if not isinstance(b, int) or b > 0:
                    pool.wait_ge(S["pv_done"], b * (CHUNKS * GROUPS) - (CHUNKS - j - 1) * GROUPS)
                pool.tensor_tensor(
                    val[:, j, :, 0:HD],
                    kvf[j % 2][:, 1, :].rearrange("p (h d) -> p h d", d=HD),
                    bv("bxv")[:, 0, :].rearrange("p (h d) -> p h d", d=HD), ALU.add).then_inc(S["val_ready"], 1)

            def steps(b, last):
                for s in range(STEPS):
                    if s > 0:
                        values(b, 2 * s - 1)
                    low_parts(b * CHUNKS + 2 * s + 1, 1)
                    if not (last and s == STEPS - 1):
                        context_low(b, 2 * s + 3)
                    values(b, 2 * s)
                    if not (last and s == STEPS - 1):
                        low_parts(b * CHUNKS + 2 * s + 2, 0)
                    if not (last and s >= STEPS - 2):
                        context_low(b, 2 * s + 4)
                values(b, CHUNKS - 1)

            context_low(0, 0)
            context_low(0, 1)
            low_parts(0, 0)
            context_low(0, 2)
            steps(0, False)
            with pool.Fori(1, BLOCKS - 1, 1) as b:
                steps(b, False)
            steps(BLOCKS - 1, True)

        @block.scalar
        def _(act):
            def context_high(b, j):
                n = b * CHUNKS + j
                act.wait_ge(S[f"ld_ctx{j % CHUNKS // HALF}"], (b + j // CHUNKS) * 16 + 16)
                if not isinstance(b, int) or n >= 2:
                    act.wait_ge(S["kv_done"], n - 1)
                act.activation(cparts[j % 2][:, 0, :, :], ctxT[:, j % CHUNKS, :, :], ACT.Copy
                               ).then_inc(S["ch_ready"], 1)

            act.wait_ge(S["ld_kv"], 32)
            for i, name in enumerate(("xk", "xv")):
                last = act.activation(wkv[:, 0, :, i * D:(i + 1) * D], w[name][:, :, :], ACT.Copy)
            last.then_inc(S["act_wkvh"], 1)
            context_high(0, 0)
            context_high(0, 1)
            act.wait_ge(S["pe_qT"], GROUPS)
            for g in (1, 3):
                act.activation(qmat[0:96, GH * g:GH * (g + 1), :],
                               B[2 + g][0:96, :].rearrange("p (h q) -> p h q", q=P), ACT.Copy
                               ).then_inc(S["act_qmat"], 1)

            def high_parts(n, i):
                act.wait_ge(S["kvf_ready"], n + 1)
                if not isinstance(n, int) or n >= 2:
                    act.wait_ge(S["kt_done"], 2 * n - 2)
                for seg in (0, 2):
                    last = act.activation(kparts[i][:, :, 32 * seg:32 * seg + 32],
                                          kvf[i][:, 0, :].rearrange("p (a c) -> p a c", c=32), ACT.Copy)
                last.then_inc(S["kh_ready"], 1)

            def exponentials(c, k):
                for k in (k, k + 1):
                    n = c * (CHUNKS * GROUPS) + k
                    act.wait_ge(S["sc_done"], n + 1)
                    if k >= GROUPS:
                        act.wait_ge(S["pv_done"], n - (GROUPS - 1))
                    act.activation(probs[k % GROUPS][:, :, :],
                                   sc_bank[k % 3][:, :].rearrange("p (h q) -> p h q", q=P), ACT.Exp
                                   ).then_inc(S["exp_ready"], 1)

            def steps(b, first, last):
                for s in range(STEPS):
                    if not first:
                        exponentials(b - 1, 8 * s)
                        exponentials(b - 1, 8 * s + 2)
                    high_parts(b * CHUNKS + 2 * s + 1, 1)
                    if not (last and s == STEPS - 1):
                        context_high(b, 2 * s + 3)
                    if not first:
                        exponentials(b - 1, 8 * s + 4)
                        exponentials(b - 1, 8 * s + 6)
                    if not (last and s == STEPS - 1):
                        high_parts(b * CHUNKS + 2 * s + 2, 0)
                    if not (last and s >= STEPS - 2):
                        context_high(b, 2 * s + 4)

            act.wait_ge(S["pool_setup"], 1)
            high_parts(0, 0)
            context_high(0, 2)
            steps(0, True, False)
            with act.Fori(1, BLOCKS - 1, 1) as b:
                steps(b, False, False)
            steps(BLOCKS - 1, False, True)
            for k in range(0, CHUNKS * GROUPS, 2):
                exponentials(BLOCKS - 1, k)

            act.wait_ge(S["dve_dmax"], 1)
            act.activation(bmax[:, :, :], bmax[:, :, :], ACT.Exp).then_inc(S["act_bw"], 1)
            act.wait_ge(S["dve_a_neg"], 1)
            act.activation(tc[:, :], tc[:, :], ACT.Exp)
            act.activation(tb[:, D:2 * D], tb[:, D:2 * D], ACT.Exp, scale=-1.0).then_inc(S["act_a_exp"], 1)
            for g in range(GROUPS):
                act.wait_ge(S["dve_c_sub"], g + 1)
                act.activation(sm[:, GH * g:GH * (g + 1), :], sm[:, GH * g:GH * (g + 1), :], ACT.Exp,
                               scale=SCALE).then_inc(S["act_c_exp"], 1)
            for g in (1, 3):
                act.wait_ge(S["pe_c_pT"], g + 1)
                act.activation(pT[:, GH * g:GH * (g + 1), :],
                               B[g][:, :].rearrange("p (h q) -> p h q", q=P), ACT.Copy).then_inc(S["act_c_pT"], 1)
            act.wait_ge(S["dve_m_sub"], 1)
            act.activation(small[:, 8:16], small[:, 8:16], ACT.Exp).then_inc(S["act_m_exp"], 1)

            def expert(e, i):
                act.wait_ge(S["pe_m_h"], e + 1)
                if not isinstance(e, int) or e >= 2:
                    act.wait_ge(S["dve_m_g"], e - 1)
                act.activation(sig[i], B[i][:, :], ACT.Sigmoid).then_inc(S["act_m_sig"], 1)
                act.wait_ge(S["pe_m_gT"], e + 1)
                if not isinstance(e, int) or e >= 2:
                    act.wait_ge(S["pe_m_down"], e - 1)
                act.activation(gT[i], B[4 + i][:, :], ACT.Copy).then_inc(S["act_m_gT"], 1)

            sig = [sm[:, 4 * i:4 * i + 4, :].rearrange("p a b -> p (a b)") for i in range(2)]
            gT = [pT[:, 4 * i:4 * i + 4, :].rearrange("p a b -> p (a b)") for i in range(2)]
            for i in range(2):
                expert(i, i)
            with act.Fori(1, EXPERTS // 2, 1) as m:
                for i in range(2):
                    expert(m * 2 + i, i)

        @block.tensor
        def _(pe):
            def transpose_d(src, bank, done):
                for c in range(DC):
                    last = pe.transpose(bank[:, c * P:(c + 1) * P], src[:, c * P:(c + 1) * P], ident)
                last.then_inc(S[done], 1)

            def project(srcT, names, bank):
                for i, name in enumerate(names):
                    for c in range(DC):
                        last = pe.matmul(bank[:, i * D:(i + 1) * D], srcT[:, c, :], w[name][:, c, :],
                                         start=(c == 0), stop=(c == DC - 1))
                return last

            pe.wait_ge(S["ld_const"], 16)
            pe.wait_ge(S["dve_xn"], 1)
            transpose_d(xn, B[0], "pe_xnT")
            pe.wait_ge(S["dve_xnT"], 1)
            pe.wait_ge(S["ld_q"], 16 * (1 + len(BIASES)))
            project(xnT, ["xq"], B[1]).then_inc(S["pe_q"], 1)
            pe.wait_ge(S["dve_qparts"], 1)
            pe.wait_ge(S["dve_ident"], 1)
            pe.wait_ge(S["pool_setup"], 1)
            for g in range(GROUPS):
                for h in range(GH):
                    last = pe.transpose(B[2 + g][0:96, h * P:(h + 1) * P].bitcast(F32R), qparts[:, GH * g + h, :],
                                        ident_r[:, :])
                last.then_inc(S["pe_qT"], 1)

            def keys_values(b, j):
                n = b * CHUNKS + j
                pe.wait_ge(S["cl_ready"], n + 1)
                if not isinstance(b, int) or n >= 1:
                    pe.wait_ge(S["kvf_ready"], n)
                products = [(a, v, c) for a, v in ((0, 0), (1, 0), (0, 1)) for c in range(DC)]
                for i, (a, v, c) in enumerate(products):
                    last = pe.matmul(kv_bank[:, :], cparts[j % 2][:, a, c, :], wkv[:, v, c, :],
                                     start=(i == 0), stop=(i == len(products) - 1))
                last.then_inc(S["kv_done"], 1)

            def turn_keys(b, j, u):
                n = b * CHUNKS + j
                if u == 0:
                    pe.wait_ge(S["kl_ready"], n + 1)
                if u == 1 or not isinstance(b, int) or n > 0:
                    pe.wait_ge(S["kt_ready"], 2 * n + u)
                for p in range(PAIRS // 2):
                    last = pe.transpose(kt_bank[:, p * P:(p + 1) * P].bitcast(F32R),
                                        kparts[j % 2][:, u * (PAIRS // 2) + p, :], ident_r[:, :])
                last.then_inc(S["kt_done"], 1)

            def max_scores(b, s, v):
                m = b * (8 * STEPS) + (8 * s + v)
                pe.wait_ge(S["kt_ready"], b * (2 * CHUNKS) + 4 * s + (3 if v < 4 else 4))
                if not isinstance(b, int) or m >= 2:
                    pe.wait_ge(S["mx_read"], m - 1)
                for a in range(2):
                    last = pe.matmul(mx_bank[v % 2][:, a * 2 * P:(a + 1) * 2 * P], qmat[0:96, 2 * v + a, :],
                                     kT[0:96, s, v, :], start=True, stop=True)
                last.then_inc(S["mx_done"], 1)

            def turn_max(b):
                pe.wait_ge(S["mparts_ready"], b * 2 + 2)
                pe.transpose(mx_bank[0][:, 0:P].bitcast(F32R), maxparts[:, :], ident_r[:, :]).then_inc(S["mt_done"], 1)

            def scores(c, k):
                for k in (k, k + 1):
                    n, g = c * (CHUNKS * GROUPS) + k, k % GROUPS
                    if k < GROUPS:
                        pe.wait_ge(S["qmat_ready"], c * GROUPS + (g + 1))
                    if k >= 3:
                        pe.wait_ge(S["exp_ready"], n - 2)
                    j = k // GROUPS
                    for i in range(2):
                        p = 2 * g + i
                        last = pe.matmul(sc_bank[k % 3][:, i * 2 * P:(i + 1) * 2 * P],
                                         kT[:, j // 2, p, (j % 2) * P:(j % 2 + 1) * P],
                                         qmat[:, 2 * p:2 * p + 2, :], start=True, stop=True)
                    last.then_inc(S["sc_done"], 1)

            def weighted_values(c, k):
                for k in (k, k + 1):
                    j, g = k // GROUPS, k % GROUPS
                    pe.wait_ge(S["exp_ready"], c * (CHUNKS * GROUPS) + k + 1)
                    if g == 0:
                        pe.wait_ge(S["val_ready"], c * CHUNKS + (j + 1))
                    for r in range(GH):
                        last = pe.matmul(pv_bank[32 * r:32 * r + VW, g * P:(g + 1) * P], val[:, j, GH * g + r, :],
                                         probs[g][:, r, :], start=(k == 0), stop=(j == CHUNKS - 1),
                                         skip_group_check=True)
                    last.then_inc(S["pv_done"], 1)

            def quarter(b, s, i, first, last):
                k = 8 * s + 2 * i
                if not first:
                    scores(b - 1, k)
                    if k > 0:
                        weighted_values(b - 1, k - 2)
                turn_keys(b, 2 * s + i // 2, i % 2)
                ms, v = (s, 0) if i == 3 else (s - 1, 2 * i + 2)
                if ms >= 0:
                    max_scores(b, ms, v)
                if i == 0 and s > 0:
                    keys_values(b, 2 * s + 1)
                if i == 2 and not (last and s == STEPS - 1):
                    keys_values(b, 2 * s + 2)
                if ms >= 0:
                    max_scores(b, ms, v + 1)

            def steps(b, first, last):
                for s in range(STEPS):
                    for i in range(4):
                        quarter(b, s, i, first, last)
                max_scores(b, STEPS - 1, 2)
                max_scores(b, STEPS - 1, 3)
                if not first:
                    weighted_values(b - 1, 8 * STEPS - 2)
                max_scores(b, STEPS - 1, 4)
                max_scores(b, STEPS - 1, 5)
                if not last:
                    keys_values(b, CHUNKS + 1)
                max_scores(b, STEPS - 1, 6)
                max_scores(b, STEPS - 1, 7)
                turn_max(b)

            pe.wait_ge(S["dve_wkvl"], 2)
            pe.wait_ge(S["dve_pvzero"], 1)
            pe.wait_ge(S["dve_qmat"], 2)
            pe.wait_ge(S["act_qmat"], 2)
            keys_values(0, 0)
            keys_values(0, 1)
            steps(0, True, False)
            with pe.Fori(1, BLOCKS - 1, 1) as b:
                steps(b, False, False)
            steps(BLOCKS - 1, False, True)
            for k in range(0, 8 * STEPS, 2):
                scores(BLOCKS - 1, k)
                if k > 0:
                    weighted_values(BLOCKS - 1, k - 2)
            weighted_values(BLOCKS - 1, 8 * STEPS - 2)

            pe.wait_ge(S["part_ready"], BLOCKS)
            for b in range(BLOCKS):
                if b >= 2:
                    pe.wait_ge(S["dve_partT_read"], b - 1)
                for g in range(GROUPS):
                    last = pe.transpose(B[5 + b % 2][:, g * P:(g + 1) * P], parts[:, b, g * P:(g + 1) * P], ident)
                last.then_inc(S["pe_partT"], 1)
            pe.wait_ge(S["dve_att"], 1)
            transpose_d(xn, B[0], "pe_attT")
            pe.wait_ge(S["dve_attT"], 1)
            pe.wait_ge(S["ld_small"], 16 * (len(WEIGHTS) - 3 + 2))
            project(xnT, ["xo"], B[1]).then_inc(S["pe_xo"], 1)

            pe.wait_ge(S["dve_a_xn"], 1)
            transpose_d(xn, B[0], "pe_a_xnT")
            pe.wait_ge(S["dve_a_xnT"], 1)
            project(xnT, ["aq", "ak"], B[1]).then_inc(S["pe_a_proj"], 1)
            project(xnT, ["av", "ag"], B[2]).then_inc(S["pe_a_proj"], 1)
            pe.wait_ge(S["dve_a_qkv"], 1)
            transpose_d(ta, B[3], "pe_a_qT")
            for c in range(DC):
                pe.matmul(B[4][:, c * D:c * D + P], ta[:, D + c * P:D + (c + 1) * P], tb[:, c * P:(c + 1) * P],
                          start=True, stop=True)
                last = pe.matmul(B[4][:, c * D + P:c * D + P + 1], ta[:, D + c * P:D + (c + 1) * P], ones[:, :],
                                 start=True, stop=True)
            last.then_inc(S["pe_a_kv"], 1)
            pe.wait_ge(S["dve_a_kvr"], 1)
            for c in range(DC):
                last = pe.matmul(B[5][:, c * D:c * D + P + H // DC], xnT[:, c, :], kvr[:, c, :], start=True, stop=True)
            last.then_inc(S["pe_a_num"], 1)
            pe.wait_ge(S["dve_a_out"], 1)
            transpose_d(xn, B[0], "pe_a_outT")
            pe.wait_ge(S["dve_a_outT"], 1)
            project(xnT, ["ao"], B[1]).then_inc(S["pe_a_o"], 1)

            pe.wait_ge(S["dve_c_xn"], 1)
            transpose_d(xn, B[0], "pe_c_xnT")
            pe.wait_ge(S["dve_c_xnT"], 1)
            project(xnT, ["fq", "fk"], B[1]).then_inc(S["pe_c_proj"], 1)
            project(xnT, ["fv"], B[2]).then_inc(S["pe_c_proj"], 1)
            pe.wait_ge(S["dve_c_qk"], 1)
            for c in range(2 * DC):
                last = pe.transpose(B[3][:, c * P:(c + 1) * P], ta[:, c * P:(c + 1) * P], ident)
            last.then_inc(S["pe_c_qkT"], 1)
            for c in range(DC):
                pe.wait_ge(S["dve_c_kbd"], c + 1)
                for u in range(2):
                    pe.matmul(B[4 + 2 * c + u][:, :], xnT[:, c, :], kbd[:, c, GH * u:GH * (u + 1), :],
                              start=True, stop=True).then_inc(S["pe_c_scores"], 1)
            for g in range(GROUPS):
                pe.wait_ge(S["act_c_exp"], g + 1)
                for h in range(GH):
                    last = pe.transpose(B[g][:, h * P:(h + 1) * P], sm[:, GH * g + h, :], ident)
                last.then_inc(S["pe_c_pT"], 1)
            pe.wait_ge(S["dve_c_pT"], 2)
            pe.wait_ge(S["act_c_pT"], 2)
            for g in range(GROUPS):
                for r in range(GH):
                    last = pe.matmul(B[4][32 * r:32 * r + VW, g * P:(g + 1) * P], vaug[:, GH * g + r, :],
                                     pT[:, GH * g + r, :], start=True, stop=True)
            last.then_inc(S["pe_c_pv"], 1)
            pe.wait_ge(S["dve_c_oT"], 1)
            for g in range(GROUPS):
                last = pe.transpose(B[5][:, g * P:(g + 1) * P], oT[:, g, :], ident)
            last.then_inc(S["pe_c_o"], 1)
            pe.wait_ge(S["dve_c_att"], 1)
            transpose_d(xn, B[0], "pe_c_attT")
            pe.wait_ge(S["dve_c_attT"], 1)
            project(xnT, ["fo"], B[1]).then_inc(S["pe_c_proj_o"], 1)

            pe.wait_ge(S["dve_m_t"], 1)
            transpose_d(xn, B[0], "pe_m_tT")
            pe.wait_ge(S["dve_m_tT"], 1)
            for c in range(DC):
                last = pe.matmul(B[7][:, 0:EXPERTS], xnT[:, c, :], router[:, c, :], start=(c == 0), stop=(c == DC - 1))
            last.then_inc(S["pe_m_logits"], 1)

            def up(m, i):
                e = m * 2 + i
                pe.wait_ge(S["experts_loaded"], m + 1)
                if not isinstance(e, int) or e >= 2:
                    pe.wait_ge(S["dve_m_g"], e - 1)
                for bank, big in ((B[i], w1), (B[2 + i], w3)):
                    for c in range(DC):
                        last = pe.matmul(bank[:, :], xnT[:, c, :], big[:, e, c, :], start=(c == 0), stop=(c == DC - 1))
                last.then_inc(S["pe_m_h"], 1)

            def turn(e, i):
                pe.wait_ge(S["dve_m_g"], e + 1)
                if not isinstance(e, int) or e >= 2:
                    pe.wait_ge(S["act_m_gT"], e - 1)
                for k in range(IC):
                    last = pe.transpose(B[4 + i][:, k * P:(k + 1) * P], sm[:, 8 + 4 * i + k, :], ident)
                last.then_inc(S["pe_m_gT"], 1)

            def down(e, i, first, final):
                pe.wait_ge(S["act_m_gT"], e + 1)

                for k in range(IC):
                    last = pe.matmul(B[6][:, 0:D], pT[:, 4 * i + k, :], w2[:, e, k, :],
                                     start=(first and k == 0), stop=(final and k == IC - 1))
                last.then_inc(S["pe_m_down"], 1)
                if final:
                    return last

            up(0, 0)
            up(0, 1)
            turn(0, 0)
            down(0, 0, True, False)
            with pe.Fori(1, EXPERTS // 2, 1) as m:
                up(m, 0)
                turn(m * 2 - 1, 1)
                down(m * 2 - 1, 1, False, False)
                up(m, 1)
                turn(m * 2, 0)
                down(m * 2, 0, False, False)
            turn(EXPERTS - 1, 1)
            down(EXPERTS - 1, 1, False, True)

        @block.vector
        def _(dve):
            links = [0]

            def link(ins):
                links[0] += 1
                ins.then_inc(S["dve_chain"], 1)
                dve.wait_ge(S["dve_chain"], links[0])

            def rsqrt(v, y, tmp):
                link(dve.tensor_scalar(tmp.bitcast(I32), v.bitcast(I32), 1, None, ALU.logical_shift_right))
                link(dve.tensor_scalar(y.bitcast(I32), tmp.bitcast(I32), -1.0, float(0x5F3759DF), ALU.mult, ALU.add))
                for _ in range(3):
                    link(dve.scalar_tensor_tensor(tmp, y, y, v, ALU.mult, ALU.mult))
                    link(dve.tensor_scalar(tmp, tmp, -0.5, 1.5, ALU.mult, ALU.add))
                    link(dve.tensor_tensor(y, y, tmp, ALU.mult))

            def layernorm(dst, src):
                link(dve.bn_stats(small[:, 0:6], src))
                link(dve.bn_aggr(small[:, 6:8], small[:, 0:6]))
                link(dve.tensor_scalar(small[:, 7:8], small[:, 7:8], EPS_LN, None, ALU.add))
                rsqrt(small[:, 7:8], small[:, 8:9], small[:, 9:10])
                return dve.tensor_scalar(dst, src, small[:, 6:7], small[:, 8:9], ALU.subtract, ALU.mult)

            def rmsnorm(dst, src, weight, tmp):
                link(dve.tensor_tensor(tmp, src, src, ALU.mult))
                link(dve.tensor_reduce(small[:, 0:1], tmp, AX_X, ALU.add))
                link(dve.tensor_scalar(small[:, 1:2], small[:, 0:1], 1.0 / D, EPS_RMS, ALU.mult, ALU.add))
                rsqrt(small[:, 1:2], small[:, 2:3], small[:, 3:4])
                return dve.scalar_tensor_tensor(dst, src, small[:, 2:3], weight, ALU.mult, ALU.mult)

            def turned(dst, bank, pe_signal, signal):
                dve.wait_ge(S[pe_signal], 1)
                dve.tensor_copy(dst[:, :, :], bank[:, 0:D].rearrange("p (c n) -> p c n", n=P)).then_inc(S[signal], 1)

            link(dve.memset(pv_bank[:, :], 0.0))
            dve.wait_ge(S["ld_x"], 16)
            layernorm(xn[:, :], x[:, :]).then_inc(S["dve_xn"], 1)
            dve.wait_ge(S["ld_const"], 16)
            dve.tensor_copy(ident_r[:, :], ident).then_inc(S["dve_ident"], 1)
            turned(xnT, B[0], "pe_xnT", "dve_xnT")
            dve.wait_ge(S["ld_q"], 16 * (1 + len(BIASES)))
            dve.memset(kbias[:, 1, :], 0.0)
            link(dve.tensor_copy(kbias[:, 0, :], bv("bxk")[:, 0, :]))
            dve.wait_ge(S["pe_q"], 1)
            q = kvf[0][:, 0, :]
            link(dve.tensor_tensor(q, B[1][:, 0:D], bv("bxq")[:, 0, :], ALU.add))
            dve.wait_ge(S["pool_setup"], 1)
            q4 = q.rearrange("p (m a d) -> p m a d", a=2, d=HD)
            qp4 = qparts[:, :, :].rearrange("p (m a) c -> p m a c", a=2)
            for seg in (0, 32):
                for a in range(2):
                    last = dve.tensor_scalar(qp4[:, :, a, seg + HD * a:seg + HD * (a + 1)], q4[:, :, a, :],
                                             SCALE, None, ALU.mult)
            link(last)
            for a in range(2):
                last = dve.scalar_tensor_tensor(qp4[:, :, a, 64 + HD * a:64 + HD * (a + 1)], q4[:, :, a, :], SCALE,
                                                qp4[:, :, a, HD * a:HD * (a + 1)].bitcast(F32), ALU.mult, ALU.subtract)
            last.then_inc(S["dve_qparts"], 1)
            for g in (0, 2):
                dve.wait_ge(S["pe_qT"], g + 1)
                dve.tensor_copy(qmat[0:96, GH * g:GH * (g + 1), :],
                                B[2 + g][0:96, :].rearrange("p (h q) -> p h q", q=P)).then_inc(S["dve_qmat"], 1)
            dve.wait_ge(S["act_qmat"], 2)
            dve.memset(pv_bank[:, :], 0.0).then_inc(S["dve_pvzero"], 1)

            dve.wait_ge(S["act_wkvh"], 1)
            for i, name in enumerate(("xk", "xv")):
                dve.tensor_tensor(wkv[:, 1, :, i * D:(i + 1) * D], w[name][:, :, :],
                                  wkv[:, 0, :, i * D:(i + 1) * D].bitcast(F32), ALU.subtract
                                  ).then_inc(S["dve_wkvl"], 1)

            def kv_out(n, i):
                dve.wait_ge(S["kv_done"], n + 1)
                if not isinstance(n, int) or n >= 2:
                    dve.wait_ge(S["val_ready"], n - 1)
                    dve.wait_ge(S["kl_ready"], n - 1)
                dve.tensor_tensor(kvf[i][:, :, :], kv_bank[:, :].rearrange("p (s n) -> p s n", s=2),
                                  kbias[:, :, :], ALU.add).then_inc(S["kvf_ready"], 1)

            def keys_out(b, j, u):
                dve.wait_ge(S["kt_done"], b * (2 * CHUNKS) + (2 * j + u + 1))
                dve.tensor_copy(kT[:, j // 2, 4 * u:4 * u + 4, (j % 2) * P:(j % 2 + 1) * P],
                                kt_bank[:, :].rearrange("p (a k) -> p a k", k=P)).then_inc(S["kt_ready"], 1)

            def step_max(b, s, v):
                dve.wait_ge(S["mx_done"], b * (8 * STEPS) + (8 * s + v + 1))
                dve.tensor_reduce(stepmax[:, s, 2 * v:2 * v + 2],
                                  mx_bank[v % 2][:, :].rearrange("p (a k) -> p a k", a=2), AX_X, ALU.max
                                  ).then_inc(S["mx_read"], 1)

            def block_max(b):
                dve.wait_ge(S["mx_read"], b * (8 * STEPS) + 8 * STEPS)
                dve.tensor_reduce(curmax[:, :], stepmax[:, :, :].rearrange("p s h -> p h s"), AX_X, ALU.max
                                  ).then_inc(S["curmax_ready"], 1)
                dve.wait_ge(S["curmax_ready"], b + 1)
                dve.tensor_scalar(maxparts[:, 96:96 + H], curmax[:, :], -1.0, None, ALU.mult
                                  ).then_inc(S["mparts_ready"], 1)
                dve.wait_ge(S["mparts_ready"], b * 2 + 1)
                dve.scalar_tensor_tensor(maxparts[:, 96 + H:P], curmax[:, :], -1.0,
                                         maxparts[:, 96:96 + H].bitcast(F32), ALU.mult, ALU.subtract
                                         ).then_inc(S["mparts_ready"], 1)
                dve.tensor_scalar(bmax[:, b, :], curmax[:, :], 1.0, None, ALU.mult).then_inc(S["bmax_ready"], 1)

            def max_rows(b, g):
                if g == 0:
                    dve.wait_ge(S["mt_done"], b + 1)
                dve.tensor_tensor(qmat[96:P, GH * g:GH * (g + 1), :],
                                  over_heads(mx_bank[0][96:P, 0:P], GH),
                                  per_head(const[96:P, C_MM + GH * g:C_MM + GH * (g + 1)], P), ALU.mult
                                  ).then_inc(S["qmat_ready"], 1)

            def part_out(c):
                dve.wait_ge(S["pv_done"], c * (CHUNKS * GROUPS) + CHUNKS * GROUPS)
                dve.tensor_scalar(parts[:, c, :], pv_bank[:, :], 1.0, None, ALU.mult).then_inc(S["part_ready"], 1)

            def quarter(b, s, i, last):
                keys_out(b, 2 * s + i // 2, i % 2)
                ms, v = (s, 0) if i == 3 else (s - 1, 2 * i + 2)
                if ms >= 0:
                    step_max(b, ms, v)
                if i == 0 and s > 0:
                    kv_out(b * CHUNKS + 2 * s + 1, 1)
                if i == 2 and not (last and s == STEPS - 1):
                    kv_out(b * CHUNKS + 2 * s + 2, 0)
                if ms >= 0:
                    step_max(b, ms, v + 1)

            def steps(b, first, last):
                for s in range(STEPS):
                    for i in range(4):
                        quarter(b, s, i, last)
                for v in range(2, 8):
                    step_max(b, STEPS - 1, v)
                block_max(b)
                max_rows(b, 0)
                max_rows(b, 1)
                if not first:
                    part_out(b - 1)
                max_rows(b, 2)
                max_rows(b, 3)
                if not last:
                    kv_out(b * CHUNKS + CHUNKS + 1, 1)

            kv_out(0, 0)
            kv_out(1, 1)
            steps(0, True, False)
            with dve.Fori(1, BLOCKS - 1, 1) as b:
                steps(b, False, False)
            steps(BLOCKS - 1, False, True)
            part_out(BLOCKS - 1)

            dve.wait_ge(S["bmax_ready"], BLOCKS)
            link(dve.tensor_reduce(small[:, 16:32], bmax[:, :, :].rearrange("p b h -> p h b"), AX_X, ALU.max))
            dve.tensor_tensor(bmax[:, :, :], bmax[:, :, :], over_heads(small[:, 16:32], BLOCKS), ALU.subtract
                              ).then_inc(S["dve_dmax"], 1)
            dve.wait_ge(S["act_bw"], 1)
            merged = ta[:, 0:H * VW].rearrange("p (h v) -> p h v", v=VW)
            piece = tb[:, 0:H * VW].rearrange("p (h v) -> p h v", v=VW)
            for b in range(BLOCKS):
                dve.wait_ge(S["pe_partT"], b + 1)
                bank = B[5 + b % 2][:, :].rearrange("p (h v) -> p h v", v=32)[:, :, 0:VW]
                ins = dve.tensor_tensor(merged if b == 0 else piece, bank, per_head(bmax[:, b, :], VW), ALU.mult)
                ins.then_inc(S["dve_partT_read"], 1)
                dve.wait_ge(S["dve_partT_read"], b + 1)
                if b:
                    link(dve.tensor_tensor(merged, merged, piece, ALU.add))
            link(dve.reciprocal(small[:, 32:48], merged[:, :, HD]))
            dve.tensor_tensor(xn[:, :].rearrange("p (h d) -> p h d", d=HD), merged[:, :, 0:HD],
                              per_head(small[:, 32:48], HD), ALU.mult).then_inc(S["dve_att"], 1)
            turned(xnT, B[0], "pe_attT", "dve_attT")
            dve.wait_ge(S["pe_xo"], 1)
            link(dve.tensor_tensor(x1[:, :], B[1][:, 0:D], bv("bxo")[:, 0, :], ALU.add))
            link(dve.tensor_tensor(x1[:, :], x1[:, :], x[:, :], ALU.add))

            layernorm(xn[:, :], x1[:, :]).then_inc(S["dve_a_xn"], 1)
            turned(xnT, B[0], "pe_a_xnT", "dve_a_xnT")
            dve.wait_ge(S["pe_a_proj"], 1)
            link(dve.tensor_tensor(ta[:, :].rearrange("p (s n) -> p s n", s=2),
                                   B[1][:, :].rearrange("p (s n) -> p s n", s=2), bv("baq", 2), ALU.add))
            dve.tensor_scalar(tc[:, :], ta[:, :], 0.0, None, ALU.min)
            dve.wait_ge(S["pe_a_proj"], 2)
            dve.tensor_tensor(tb[:, :].rearrange("p (s n) -> p s n", s=2),
                              B[2][:, :].rearrange("p (s n) -> p s n", s=2), bv("bav", 2), ALU.add
                              ).then_inc(S["dve_a_neg"], 1)
            dve.wait_ge(S["act_a_exp"], 1)
            dve.scalar_tensor_tensor(ta[:, :], ta[:, :], 0.0, tc[:, :], ALU.max, ALU.add).then_inc(S["dve_a_qkv"], 1)
            link(dve.tensor_scalar(tb[:, D:2 * D], tb[:, D:2 * D], 1.0, None, ALU.add))
            dve.reciprocal(tc[:, 0:D], tb[:, D:2 * D])
            dve.wait_ge(S["pe_a_qT"], 1)
            dve.tensor_copy(xnT[:, :, :], B[3][:, 0:D].rearrange("p (c n) -> p c n", n=P))
            dve.wait_ge(S["pe_a_kv"], 1)
            for c in range(DC):
                dve.tensor_tensor(kvr[:, c, 0:P], B[4][:, c * D:c * D + P], const[:, C_BM:C_BM + P], ALU.mult)
                last = dve.tensor_scalar(kvr[:, c, P:P + H // DC], const[:, C_HM:C_HM + H // DC],
                                         B[4][:, c * D + P:c * D + P + 1], None, ALU.mult)
            last.then_inc(S["dve_a_kvr"], 1)
            dve.wait_ge(S["pe_a_num"], 1)
            num = B[5][:, :].rearrange("p (c n) -> p c n", c=DC)
            zz = small[:, 16:32].rearrange("p (c h) -> p c h", c=DC)
            link(dve.tensor_scalar(zz, num[:, :, P:P + H // DC], EPS_Z, None, ALU.add))
            link(dve.reciprocal(small[:, 32:48], small[:, 16:32]))
            for c in range(DC):
                last = dve.tensor_tensor(ta[:, c * P:(c + 1) * P].rearrange("p (h d) -> p h d", d=HD),
                                         num[:, c, 0:P].rearrange("p (h d) -> p h d", d=HD),
                                         per_head(small[:, 32 + 8 * c:40 + 8 * c], HD), ALU.mult)
            link(last)
            dve.tensor_tensor(xn[:, :], ta[:, 0:D], tc[:, 0:D], ALU.mult).then_inc(S["dve_a_out"], 1)
            turned(xnT, B[0], "pe_a_outT", "dve_a_outT")
            dve.wait_ge(S["pe_a_o"], 1)
            link(dve.tensor_tensor(x2[:, :], B[1][:, 0:D], bv("bao")[:, 0, :], ALU.add))
            link(dve.tensor_tensor(x2[:, :], x2[:, :], x1[:, :], ALU.add))

            link(layernorm(xl[:, :], x2[:, :]))
            rmsnorm(xn[:, :], xl[:, :], bv("anw")[:, 0, :], tb[:, 0:D]).then_inc(S["dve_c_xn"], 1)
            turned(xnT, B[0], "pe_c_xnT", "dve_c_xnT")
            dve.memset(vaug[:, :, HD:VW], 1.0)
            dve.wait_ge(S["pe_c_proj"], 1)
            pairs = B[1][:, :].rearrange("p (h j e) -> p h j e", h=2 * H, e=2)
            turnedqk = ta[:, :].rearrange("p (h j e) -> p h j e", h=2 * H, e=2)
            fr = freqs[:, :].rearrange("p (j e) -> p j e", e=2)
            cos, sin = (over_heads(fr[:, :, e], 2 * H) for e in range(2))
            t0, t1, t2, t3 = (v.rearrange("p (h j) -> p h j", j=HD // 2)
                              for v in (tb[:, 0:D], tb[:, D:2 * D], tc[:, 0:D], tc[:, D:2 * D]))
            dve.tensor_tensor(t0, pairs[:, :, :, 0], cos, ALU.mult)
            dve.tensor_tensor(t1, pairs[:, :, :, 1], sin, ALU.mult)
            dve.tensor_tensor(t2, pairs[:, :, :, 0], sin, ALU.mult)
            link(dve.tensor_tensor(t3, pairs[:, :, :, 1], cos, ALU.mult))
            dve.tensor_tensor(turnedqk[:, :, :, 0], t0, t1, ALU.subtract)
            dve.tensor_tensor(turnedqk[:, :, :, 1], t2, t3, ALU.add).then_inc(S["dve_c_qk"], 1)
            dve.wait_ge(S["pe_c_proj"], 2)
            dve.tensor_copy(vaug[:, :, 0:HD], B[2][:, 0:D].rearrange("p (h d) -> p h d", d=HD))
            dve.wait_ge(S["pe_c_qkT"], 1)
            dve.tensor_copy(xnT[:, :, :], B[3][:, 0:D].rearrange("p (c n) -> p c n", n=P))
            for c in range(DC):
                dve.tensor_tensor(kbd[:, c, :, :], over_heads(B[3][:, D + c * P:D + (c + 1) * P], H // DC),
                                  per_head(const[:, C_HM:C_HM + H // DC], P), ALU.mult).then_inc(S["dve_c_kbd"], 1)
            for g in range(GROUPS):
                s4 = sm[:, GH * g:GH * (g + 1), :]
                dve.wait_ge(S["pe_c_scores"], g + 1)
                link(dve.tensor_tensor(s4, B[4 + g][:, :].rearrange("p (h k) -> p h k", k=P),
                                       over_heads(const[:, C_CA:C_CA + P], GH), ALU.add))
                link(dve.tensor_reduce(small[:, 16 + GH * g:16 + GH * (g + 1)], s4, AX_X, ALU.max))
                dve.tensor_tensor(s4, s4, per_head(small[:, 16 + GH * g:16 + GH * (g + 1)], P), ALU.subtract
                                  ).then_inc(S["dve_c_sub"], 1)
            for g in (0, 2):
                dve.wait_ge(S["pe_c_pT"], g + 1)
                dve.tensor_copy(pT[:, GH * g:GH * (g + 1), :],
                                B[g][:, :].rearrange("p (h q) -> p h q", q=P)).then_inc(S["dve_c_pT"], 1)
            dve.wait_ge(S["pe_c_pv"], 1)
            dve.tensor_copy(oT[:, :, :], B[4][:, :].rearrange("p (g q) -> p g q", q=P)).then_inc(S["dve_c_oT"], 1)
            dve.wait_ge(S["pe_c_o"], 1)
            o = B[5][:, :].rearrange("p (h v) -> p h v", v=32)
            link(dve.reciprocal(small[:, 32:48], o[:, :, HD]))
            dve.tensor_tensor(xn[:, :].rearrange("p (h d) -> p h d", d=HD), o[:, :, 0:HD],
                              per_head(small[:, 32:48], HD), ALU.mult).then_inc(S["dve_c_att"], 1)
            turned(xnT, B[0], "pe_c_attT", "dve_c_attT")
            dve.wait_ge(S["pe_c_proj_o"], 1)
            link(dve.tensor_tensor(hres[:, :], B[1][:, 0:D], xl[:, :], ALU.add))

            rmsnorm(xn[:, :], hres[:, :], bv("fnw")[:, 0, :], tb[:, 0:D]).then_inc(S["dve_m_t"], 1)
            turned(xnT, B[0], "pe_m_tT", "dve_m_tT")
            link(dve.tensor_tensor(hres[:, :], hres[:, :], x2[:, :], ALU.add))
            dve.wait_ge(S["pe_m_logits"], 1)
            E = EXPERTS
            link(dve.tensor_reduce(small[:, 0:1], B[7][:, 0:E], AX_X, ALU.max))
            dve.tensor_scalar(small[:, 8:16], B[7][:, 0:E], small[:, 0:1], None, ALU.subtract
                              ).then_inc(S["dve_m_sub"], 1)
            dve.wait_ge(S["act_m_exp"], 1)
            pr = small[:, 16:24]
            link(dve.tensor_reduce(small[:, 1:2], small[:, 8:16], AX_X, ALU.add))
            link(dve.reciprocal(small[:, 2:3], small[:, 1:2]))
            link(dve.tensor_scalar(pr, small[:, 8:16], small[:, 2:3], None, ALU.mult))
            big = small[:, 64:128].rearrange("p (a b) -> p a b", b=E)
            same = small[:, 128:192].rearrange("p (a b) -> p a b", b=E)
            dve.tensor_tensor(big, over_heads(pr, E), per_head(pr, E), ALU.is_gt)
            link(dve.tensor_tensor(same, over_heads(pr, E), per_head(pr, E), ALU.is_equal))
            link(dve.tensor_tensor(same, same, const[:, C_LT:C_LT + E * E].rearrange("p (a b) -> p a b", b=E),
                                   ALU.mult))
            link(dve.tensor_tensor(big, big, same, ALU.add))
            link(dve.tensor_reduce(small[:, 24:32], big, AX_X, ALU.add))
            link(dve.scalar_tensor_tensor(small[:, 32:40], small[:, 24:32], 1.5, pr, ALU.is_lt, ALU.mult))
            link(dve.tensor_reduce(small[:, 3:4], small[:, 32:40], AX_X, ALU.add))
            link(dve.reciprocal(small[:, 4:5], small[:, 3:4]))
            link(dve.tensor_scalar(share[:, :, 0], small[:, 32:40], small[:, 4:5], None, ALU.mult))

            def gated(e, i):
                sig = sm[:, 4 * i:4 * i + 4, :].rearrange("p a b -> p (a b)")
                g = sm[:, 8 + 4 * i:12 + 4 * i, :].rearrange("p a b -> p (a b)")
                dve.wait_ge(S["act_m_sig"], e + 1)
                if not isinstance(e, int) or e >= 2:
                    dve.wait_ge(S["pe_m_gT"], e - 1)
                dve.tensor_tensor(sig, sig, B[i][:, :], ALU.mult).then_inc(S["dve_m_w"], 1)
                dve.wait_ge(S["dve_m_w"], e + 1)
                dve.scalar_tensor_tensor(g, sig, share[:, e, :], B[2 + i][:, :], ALU.mult, ALU.mult
                                         ).then_inc(S["dve_m_g"], 1)

            gated(0, 0)
            gated(1, 1)
            with dve.Fori(1, EXPERTS // 2, 1) as m:
                gated(m * 2, 0)
                gated(m * 2 + 1, 1)
            dve.wait_ge(S["pe_m_down"], EXPERTS)
            dve.tensor_tensor(fin[:, :], B[6][:, 0:D], hres[:, :], ALU.add).then_inc(S["dve_fin"], 1)


MATRICES = {"w_xq": ("L0_xattn_Wq", True), "w_xk": ("L0_xattn_Wk", True), "w_xv": ("L0_xattn_Wv", True),
            "w_xo": ("L0_xattn_Wo", True), "w_aq": ("L0_attn_wq_w", False), "w_ak": ("L0_attn_wk_w", False),
            "w_av": ("L0_attn_wv_w", False), "w_ag": ("L0_attn_wg_w", False), "w_ao": ("L0_attn_out_w", False),
            "w_fq": ("L0_ffn_wq", False), "w_fk": ("L0_ffn_wk", False), "w_fv": ("L0_ffn_wv", False),
            "w_fo": ("L0_ffn_wo", False), "router": ("L0_ffn_router_w", False), "freqs": ("L0_ffn_freqs_cis", False),
            "w1": ("L0_ffn_w1", False), "w3": ("L0_ffn_w3", False), "w2": ("L0_ffn_w2", False)}
VECTORS = {"bxq": "L0_xattn_bq", "bxk": "L0_xattn_bk", "bxv": "L0_xattn_bv", "bxo": "L0_xattn_bo",
           "baq": "L0_attn_wq_b", "bak": "L0_attn_wk_b", "bav": "L0_attn_wv_b", "bag": "L0_attn_wg_b",
           "bao": "L0_attn_out_b", "anw": "L0_ffn_attn_norm_w", "fnw": "L0_ffn_ffn_norm_w"}


def constants(np):
    c = np.zeros((P, C_N), np.float32)
    i = np.arange(P)
    c[:, C_ID:C_ID + P] = np.eye(P)
    c[:, C_BM:C_BM + P] = i[:, None] // HD == i[None, :] // HD
    c[:, C_CA:C_CA + P] = np.where(i[:, None] >= i[None, :], 0.0, MASKED)
    c[:, C_HM:C_HM + P // HD] = i[:, None] // HD == np.arange(P // HD)[None, :]
    c[96:, C_MM:C_MM + H] = np.arange(32)[:, None] % H == np.arange(H)[None, :]
    e = np.arange(EXPERTS)
    c[:, C_LT:] = (e[None, :] < e[:, None]).reshape(1, -1)
    return c


def kernel(**inputs):
    import numpy as np
    import concourse.bacc as bacc
    from concourse.bass_utils import run_bass_kernel_spmd

    nc = bacc.Bacc("TRN2", target_bir_lowering=False, num_devices=1)
    arrays = {"x": np.asarray(inputs["x"]).reshape(P, D), "const": constants(np)}
    c = np.asarray(inputs["ctx_1024"]).reshape(BLOCKS, 2, HALF, P, DC, P)
    arrays["ctxT"] = c.transpose(0, 1, 5, 2, 4, 3).reshape(BLOCKS, 2, P, HALF * DC * P)
    for name, (given, turned) in MATRICES.items():
        a = np.asarray(inputs[given])
        arrays[name] = a.T if turned else a
    for name, given in VECTORS.items():
        arrays[name] = np.asarray(inputs[given])
    arrays = {n: np.ascontiguousarray(a) for n, a in arrays.items()}
    dr = {n: nc.dram_tensor(f"in_{n}", a.shape, mybir.dt.from_np(a.dtype), kind="ExternalInput").ap()
          for n, a in arrays.items()}
    out = nc.dram_tensor("out", (P, D), F32, kind="ExternalOutput").ap()
    perceiver_layer(nc, dr, out)
    r = run_bass_kernel_spmd(nc, [{f"in_{n}": a for n, a in arrays.items()}], core_ids=[0])
    return r.results[0]["out"].reshape(1, P, D)
```

```python
from contextlib import ExitStack

import concourse.bass as bass
from concourse import mybir

F32 = mybir.dt.float32
F32R = mybir.dt.float32r
I32 = mybir.dt.int32
ALU = mybir.AluOpType
ACT = mybir.ActivationFunctionType
AX_X = mybir.AxisListType.X

P = 128
D = 256
DC = D // P
H = 16
HD = D // H
VW = HD + 1
PAIRS = H // 2
KEYS = 12544
BLOCKS = 7
CHUNKS = KEYS // P // BLOCKS
STEPS = CHUNKS // 2
HALF = CHUNKS // 2
GROUPS = 4
GH = H // GROUPS
EXPERTS = 8
INNER = 512
IC = INNER // P
SCALE = 0.25
MASKED = -4.0e9
EPS_LN, EPS_RMS, EPS_Z = 1e-5, 1e-6, 1e-6

WEIGHTS = ["xq", "xk", "xv", "xo", "aq", "ak", "av", "ag", "ao", "fq", "fk", "fv", "fo"]
BIASES = ["bxq", "bxk", "bxv", "bxo", "baq", "bak", "bav", "bag", "bao", "anw", "fnw"]
C_ID, C_BM, C_CA, C_HM, C_MM, C_LT = 0, 128, 256, 384, 392, 408
C_N = C_LT + EXPERTS * EXPERTS

COUNTING = [
    "ch_ready",
    "cl_ready",
    "kv_done",
    "kvf_ready",
    "kh_ready",
    "kl_ready",
    "val_ready",
    "kt_done",
    "kt_ready",
    "mx_done",
    "mx_read",
    "curmax_ready",
    "mparts_ready",
    "mt_done",
    "qmat_ready",
    "qmat1_ready",
    "bmax_ready",
    "sc_done",
    "exp_ready",
    "pv_done",
    "part_ready",
]
ONCE = [
    "pool_setup", "dve_ident", "dve_pvzero", "act_wkvh", "dve_wkvl",
    "dve_xn", "pe_xnT", "dve_xnT", "pe_q", "dve_qparts", "pe_qT", "dve_qmat", "act_qmat",
    "dve_dmax", "act_bw", "pe_partT", "dve_partT_read",
    "dve_att", "pe_attT", "dve_attT", "pe_xo",
    "dve_a_xn", "pe_a_xnT", "dve_a_xnT", "pe_a_proj", "dve_a_neg", "dve_a_vg", "act_a_exp", "dve_a_qkv",
    "pe_a_qT", "pe_a_kv", "dve_a_kvr", "pe_a_num", "dve_a_out", "pe_a_outT", "dve_a_outT", "pe_a_o",
    "dve_c_xn", "pe_c_xnT", "dve_c_xnT", "pe_c_proj", "dve_c_qk", "pe_c_qkT", "dve_c_kbd",
    "pe_c_scores", "dve_c_masked", "dve_c_max", "dve_c_sub", "act_c_qT",
    "act_c_exp", "pe_c_pT", "dve_c_pT", "act_c_pT", "pe_c_pv",
    "dve_c_oT", "pe_c_o", "dve_c_att", "pe_c_attT", "dve_c_attT", "pe_c_proj_o",
    "dve_m_t", "pe_m_tT", "dve_m_tT", "dve_m_tparts", "act_m_high", "pool_m_low", "dve_m_low",
    "pe_m_logits", "dve_m_sub", "act_m_exp", "dve_m_w",
    "pe_m_h1", "pe_m_h3", "act_m_sig", "dve_m_g", "pe_m_gT", "act_m_gT", "pe_m_down",
    "dve_fin",
]
LOADS = ["ld_first", "ld_x", "ld_const", "ld_q", "ld_kv", "ld_ctx0", "ld_ctx1", "ld_small", "ld_experts0",
         "ld_experts1", "ld_experts2", "ld_experts3", "experts_loaded", "stored"]


def perceiver_layer(nc, dr, out):
    ctx = ExitStack()
    with ctx:
        def sb(name, shape, dt=F32):
            return ctx.enter_context(nc.sbuf_tensor(name, shape, dt))

        S = {n: ctx.enter_context(nc.semaphore(n)) for n in COUNTING + ONCE + LOADS + ["dve_chain"]}

        x = sb("x_in", [P, D])
        w = {n: sb("w_" + n, [P, DC, D]) for n in WEIGHTS}
        router = sb("router", [P, DC, EXPERTS])
        bias = sb("bias", [P, len(BIASES), D])
        const = sb("const", [P, C_N])
        freqs = sb("freqs", [P, HD])
        ident_r = sb("ident_r", [P, P], F32R)
        ones = sb("ones", [P, 1])
        parts_start = (nc.sbuf_base + 31) // 32 * 32
        parts = sb("parts", [P, BLOCKS + 1, GROUPS * P])
        bmax = sb("bmax", [P, BLOCKS, H])
        small = sb("small", [P, 512])
        xn = sb("xn", [P, D])
        xnT = sb("xnT", [P, DC, P])

        ARENA = 142 * 1024
        at = [(nc.sbuf_base + 31) // 32 * 32]
        arena_end = at[0] + ARENA
        sb("arena", [P, ARENA // 4])
        arena_start = at[0]

        def place(name, shape, dt=F32):
            size = 4
            for n in shape[1:]:
                size *= n
            h = nc.alloc_sbuf_tensor_at(name, shape, dt, offset=at[0])
            at[0] += (size + 31) // 32 * 32
            assert at[0] <= arena_end, (name, at[0] - arena_end)
            return h

        kT = place("kT", [P, STEPS, PAIRS, 2 * P], F32R)
        ctxT = place("ctxT", [P, CHUNKS, DC, P])
        kparts = [place(f"kparts{i}", [P, PAIRS, P], F32R) for i in range(2)]
        val = place("val", [P, CHUNKS, H, VW])
        cparts = [place(f"cparts{i}", [P, 2, DC, P], F32R) for i in range(2)]
        wkv = place("wkv", [P, 2, DC, 2 * D], F32R)
        kvf = [place(f"kvf{i}", [P, 2, D]) for i in range(2)]
        kbias = place("kbias", [P, 2, D])
        probs = [place(f"probs{i}", [P, GH, P]) for i in range(GROUPS)]
        qmat = place("qmat", [P, H, P], F32R)
        qparts = place("qparts", [P, H, 96], F32R)
        stepmax = place("stepmax", [P, STEPS, H])
        curmax = place("curmax", [P, H])
        maxparts = place("maxparts", [P, P], F32R)

        at[0] = arena_start
        weights_start = at[0]
        w13 = [place(n, [P, EXPERTS, DC, INNER]) for n in ("w1", "w3")]
        low13 = [nc.alloc_sbuf_tensor_at(n, [P, EXPERTS, DC, INNER], F32R,
                                         offset=weights_start + i * EXPERTS * DC * INNER * 4)
                 for i, n in enumerate(("low1", "low3"))]
        high13 = nc.alloc_sbuf_tensor_at("high13", [P, 2, 2, DC, INNER], F32R, offset=parts_start)
        w2 = place("w2", [P, EXPERTS, IC, D])
        ta = place("ta", [P, 2 * D])
        tb = place("tb", [P, 2 * D])
        tc = place("tc", [P, 2 * D])
        sm = place("sm", [P, H, P])
        pT = place("pT", [P, H, P])
        kbd = place("kbd", [P, DC, H // DC, P])
        oT = place("oT", [P, GROUPS, P])
        vaug = place("vaug", [P, H, VW])
        kvr = place("kvr", [P, DC, P + H // DC])
        x1, x2, xl, hres = (place(n, [P, D]) for n in ("x1", "x2", "xl", "hres"))
        fin = place("fin", [P, D])
        share = place("share", [P, EXPERTS, 1])
        tparts = place("tparts", [P, 2, DC, P], F32R)

        B = [ctx.enter_context(nc.psum_tensor(f"bank{i}", [P, 512], F32)) for i in range(8)]
        kv_bank, kt_bank, mx_bank, sc_bank, pv_bank = B[0], B[1], B[2:4], B[4:7], B[7]

        ident = const[:, C_ID:C_ID + P]

        def kv_of(b, j):
            odd = j % 2 == 1 if isinstance(b, int) and b == 0 else j % CHUNKS == 1
            return sc_bank[2] if odd else kv_bank

        def bv(first, n=1):
            i = BIASES.index(first)
            return bias[:, i:i + n, :]

        def per_head(v, n):
            return v.unsqueeze(2).broadcast_to([v.shape[0], v.shape[1], n])

        def over_heads(v, n):
            return v.unsqueeze(1).broadcast_to([v.shape[0], n, v.shape[1]])

        block = ctx.enter_context(nc.Block())

        @block.sync
        def _(sp):
            def ctx_load(b, half):
                if not isinstance(b, int) or b > 0:
                    sp.wait_ge(S["cl_ready"], b * CHUNKS - CHUNKS + HALF * (half + 1))
                sp.dma_start(ctxT[:, HALF * half:HALF * (half + 1), :, :],
                             dr["ctxT"][b, half]).then_inc(S[f"ld_ctx{half}"], 16)

            def weight(name):
                return w[name][:, :, :], dr["w_" + name].rearrange("(c p) n -> p c n", p=P)

            sp.dma_start(x[:, :], dr["x"]).then_inc(S["ld_x"], 16)
            sp.dma_start(*weight("xk")).then_inc(S["ld_kv"], 16)
            sp.dma_start(*weight("xv")).then_inc(S["ld_kv"], 16)
            sp.dma_start(const[:, :], dr["const"]).then_inc(S["ld_const"], 16)
            first, early = 2, 3 * D
            sp.dma_start(ctxT[:, 0:first, :, :], dr["ctxT"][0, 0][:, 0:first * D]).then_inc(S["ld_first"], 16)
            sp.dma_start(*weight("xq")).then_inc(S["ld_q"], 16)
            biases = bias[:, :, :].rearrange("p n d -> p (n d)")
            sp.dma_start(biases[:, 0:early], dr["biases"][0:early].partition_broadcast(P)).then_inc(S["ld_q"], 16)
            sp.dma_start(ctxT[:, first:HALF, :, :], dr["ctxT"][0, 0][:, first * D:]).then_inc(S["ld_ctx0"], 16)
            ctx_load(0, 1)
            sp.dma_start(biases[:, early:], dr["biases"][early:].partition_broadcast(P)).then_inc(S["ld_small"], 16)
            for name in WEIGHTS[3:]:
                sp.dma_start(*weight(name)).then_inc(S["ld_small"], 16)
            sp.dma_start(router[:, :, :], dr["router"].rearrange("(c p) n -> p c n", p=P)).then_inc(S["ld_small"], 16)
            sp.dma_start(freqs[:, :], dr["freqs"][0:P, :]).then_inc(S["ld_small"], 16)
            with sp.Fori(1, BLOCKS, 1) as b:
                ctx_load(b, 0)
                ctx_load(b, 1)
            sp.wait_ge(S["pv_done"], BLOCKS * CHUNKS * GROUPS)
            sp.wait_ge(S["part_ready"], BLOCKS + 1)
            for e in range(0, EXPERTS, 2):
                for big, name in zip(w13, ("w1", "w3")):
                    for c in range(DC):
                        sp.dma_start(big[:, e:e + 2, c, :],
                                     dr[name][e:e + 2, c * P:(c + 1) * P, :].rearrange("e p n -> p e n")
                                     ).then_inc(S[f"ld_experts{e // 2}"], 16)
                for i in range(2):
                    sp.dma_start(w2[:, e + i, :, :], dr["w2"][e + i].rearrange("(c p) n -> p c n", p=P)
                                 ).then_inc(S[f"ld_experts{e // 2}"], 16)
            for m in range(EXPERTS // 2):
                sp.wait_ge(S[f"ld_experts{m}"], 16 * (2 * DC + 2))
                sp.sem_inc(S["experts_loaded"], 1)
            sp.wait_ge(S["dve_fin"], 1)
            sp.dma_start(out, fin[:, :]).then_inc(S["stored"], 16)
            sp.wait_ge(S["stored"], 16)

        @block.gpsimd
        def _(pool):
            pool.memset(ones[:, :], 1.0)
            pool.memset(val[:, :, :, HD:VW], 1.0)
            pool.memset(qparts[:, :, :].bitcast(F32), 0.0)
            pool.memset(maxparts[:, :].bitcast(F32), 0.0)
            for i in range(2):
                last = pool.memset(kparts[i][:, :, 96:P].bitcast(F32), 1.0)
            last.then_inc(S["pool_setup"], 1)
            pool.wait_ge(S["ld_q"], 32)

            def context_low(b, j):
                n = b * CHUNKS + j
                pool.wait_ge(S["ch_ready"], n + 1)
                pool.tensor_tensor(cparts[j % 2][:, 1, :, :], ctxT[:, j % CHUNKS, :, :],
                                   cparts[j % 2][:, 0, :, :].bitcast(F32), ALU.subtract
                                   ).then_inc(S["cl_ready"], 1)

            def low_parts(n, i):
                pool.wait_ge(S["kh_ready"], n + 1)
                pool.tensor_tensor(
                    kparts[i][:, :, 32:64],
                    kvf[i][:, 0, :].rearrange("p (a c) -> p a c", c=32),
                    kparts[i][:, :, 0:32].bitcast(F32), ALU.subtract).then_inc(S["kl_ready"], 1)

            def values(b, j):
                if not isinstance(b, int) or b > 0:
                    pool.wait_ge(S["pv_done"], b * (CHUNKS * GROUPS) - (CHUNKS - j - 1) * GROUPS)
                pool.tensor_tensor(
                    val[:, j, :, 0:HD],
                    kvf[j % 2][:, 1, :].rearrange("p (h d) -> p h d", d=HD),
                    bv("bxv")[:, 0, :].rearrange("p (h d) -> p h d", d=HD), ALU.add).then_inc(S["val_ready"], 1)

            def first_steps():
                for s in range(STEPS):
                    low_parts(2 * s + 1, 1)
                    values(0, 2 * s)
                    values(0, 2 * s + 1)
                    context_low(0, 2 * s + 4)
                    low_parts(2 * s + 2, 0)
                    if s < STEPS - 1:
                        context_low(0, 2 * s + 5)

            def steps(b, last):
                for s in range(STEPS):
                    if s > 0:
                        values(b, 2 * s - 1)
                    low_parts(b * CHUNKS + 2 * s + 1, 1)
                    if not (last and s == STEPS - 1):
                        context_low(b, 2 * s + 3)
                    values(b, 2 * s)
                    if not (last and s == STEPS - 1):
                        low_parts(b * CHUNKS + 2 * s + 2, 0)
                    if not (last and s >= STEPS - 2):
                        context_low(b, 2 * s + 4)
                values(b, CHUNKS - 1)

            context_low(0, 0)
            context_low(0, 1)
            low_parts(0, 0)
            context_low(0, 2)
            context_low(0, 3)
            first_steps()
            with pool.Fori(1, BLOCKS - 1, 1) as b:
                steps(b, False)
            steps(BLOCKS - 1, True)

            for e in range(2):
                for which in range(2):
                    pool.wait_ge(S["act_m_high"], 2 * e + which + 1)
                    for c in range(DC):
                        last = pool.tensor_tensor(low13[which][:, e, c, :], w13[which][:, e, c, :],
                                                  high13[:, e, which, c, :].bitcast(F32), ALU.subtract)
                    last.then_inc(S["pool_m_low"], 1)

        @block.scalar
        def _(act):
            def context_high(b, j):
                n = b * CHUNKS + j
                if isinstance(b, int) and n < 2:
                    act.wait_ge(S["ld_first"], 16)
                else:
                    act.wait_ge(S[f"ld_ctx{j % CHUNKS // HALF}"], (b + j // CHUNKS) * 16 + 16)
                if not isinstance(b, int) or n >= 2:
                    act.wait_ge(S["kv_done"], n - 1)
                act.activation(cparts[j % 2][:, 0, :, :], ctxT[:, j % CHUNKS, :, :], ACT.Copy
                               ).then_inc(S["ch_ready"], 1)

            act.wait_ge(S["ld_kv"], 32)
            for i, name in enumerate(("xk", "xv")):
                last = act.activation(wkv[:, 0, :, i * D:(i + 1) * D], w[name][:, :, :], ACT.Copy)
            last.then_inc(S["act_wkvh"], 1)
            context_high(0, 0)
            context_high(0, 1)
            act.wait_ge(S["pe_qT"], GROUPS)
            for g in (1, 3):
                act.activation(qmat[0:96, GH * g:GH * (g + 1), :],
                               B[2 + g][0:96, :].rearrange("p (h q) -> p h q", q=P), ACT.Copy
                               ).then_inc(S["act_qmat"], 1)

            def high_parts(n, i):
                act.wait_ge(S["kvf_ready"], n + 1)
                if not isinstance(n, int) or n >= 2:
                    act.wait_ge(S["kt_done"], 2 * n - 2)
                for seg in (0, 2):
                    last = act.activation(kparts[i][:, :, 32 * seg:32 * seg + 32],
                                          kvf[i][:, 0, :].rearrange("p (a c) -> p a c", c=32), ACT.Copy)
                last.then_inc(S["kh_ready"], 1)

            def keys_out(b, j, u):
                act.wait_ge(S["kt_done"], b * (2 * CHUNKS) + (2 * j + u + 1))
                act.activation(kT[:, j // 2, 4 * u:4 * u + 4, (j % 2) * P:(j % 2 + 1) * P],
                               kt_bank[:, :].rearrange("p (a k) -> p a k", k=P), ACT.Copy).then_inc(S["kt_ready"], 1)

            def max_rows(b):
                for h in range(GH, 2 * GH):
                    if h == GH:
                        act.wait_ge(S["mt_done"], b * 2 + 2)
                    last = act.activation(qmat[96:P, h, :], mx_bank[1][96:P, 0:P], ACT.Copy,
                                          scale=const[96:P, C_MM + h:C_MM + h + 1])
                last.then_inc(S["qmat1_ready"], 1)

            def part_out(c):
                act.activation(parts[:, c, :], pv_bank[:, :], ACT.Copy).then_inc(S["part_ready"], 1)

            def exponential(c, k):
                n = c * (CHUNKS * GROUPS) + k
                act.wait_ge(S["sc_done"], n + 1)
                if k >= GROUPS:
                    act.wait_ge(S["pv_done"], n - (GROUPS - 1))
                act.activation(probs[k % GROUPS][:, :, :],
                               sc_bank[k % 3][:, :].rearrange("p (h q) -> p h q", q=P), ACT.Exp
                               ).then_inc(S["exp_ready"], 1)

            def first_steps():
                for s in range(STEPS):
                    high_parts(2 * s + 1, 1)
                    context_high(0, 2 * s + 4)
                    keys_out(0, 2 * s, 0)
                    keys_out(0, 2 * s, 1)
                    high_parts(2 * s + 2, 0)
                    keys_out(0, 2 * s + 1, 0)
                    if s < STEPS - 1:
                        context_high(0, 2 * s + 5)
                    keys_out(0, 2 * s + 1, 1)
                max_rows(0)

            def steps(b, last):
                for s in range(STEPS):
                    k = 8 * s
                    exponential(b - 1, k)
                    if s == 0:
                        part_out(b - 1)
                    exponential(b - 1, k + 1)
                    if s > 0:
                        exponential(b - 1, k + 2)
                    high_parts(b * CHUNKS + 2 * s + 1, 1)
                    if s == 0:
                        exponential(b - 1, k + 2)
                    exponential(b - 1, k + 3)
                    if not (last and s == STEPS - 1):
                        context_high(b, 2 * s + 3)
                    for i in range(4, 7):
                        exponential(b - 1, k + i)
                    if s == STEPS - 1:
                        keys_out(b, CHUNKS - 1, 1)
                    if not (last and s == STEPS - 1):
                        high_parts(b * CHUNKS + 2 * s + 2, 0)
                    exponential(b - 1, k + 7)
                    if not (last and s >= STEPS - 2):
                        context_high(b, 2 * s + 4)
                max_rows(b)

            act.wait_ge(S["pool_setup"], 1)
            high_parts(0, 0)
            context_high(0, 2)
            context_high(0, 3)
            first_steps()
            with act.Fori(1, BLOCKS - 1, 1) as b:
                steps(b, False)
            steps(BLOCKS - 1, True)
            for k in range(CHUNKS * GROUPS):
                exponential(BLOCKS - 1, k)
                if k == 0:
                    part_out(BLOCKS - 1)
                if k == 1:
                    act.wait_ge(S["dve_dmax"], 1)
                    act.activation(bmax[:, :, :], bmax[:, :, :], ACT.Exp).then_inc(S["act_bw"], 1)
            act.wait_ge(S["pv_done"], BLOCKS * CHUNKS * GROUPS)
            part_out(BLOCKS)

            act.wait_ge(S["dve_a_neg"], 1)
            act.activation(tc[:, :], tc[:, :], ACT.Exp).then_inc(S["act_a_exp"], 1)
            act.wait_ge(S["dve_a_vg"], 1)
            act.activation(tb[:, D:2 * D], tb[:, D:2 * D], ACT.Exp, scale=-1.0).then_inc(S["act_a_exp"], 1)
            act.wait_ge(S["pe_c_qkT"], 2)
            act.activation(xnT[:, :, :], B[5][:, 0:D].rearrange("p (c n) -> p c n", n=P), ACT.Copy
                           ).then_inc(S["act_c_qT"], 1)
            for g in range(GROUPS):
                act.wait_ge(S["dve_c_sub"], g + 1)
                for h in range(GH * g, GH * (g + 1)):
                    last = act.activation(sm[:, h, :], sm[:, h, :], ACT.Exp, scale=SCALE,
                                          bias=small[:, 48 + h:49 + h])
                last.then_inc(S["act_c_exp"], 1)
            for g in (1, 3):
                act.wait_ge(S["pe_c_pT"], g + 1)
                act.activation(pT[:, GH * g:GH * (g + 1), :],
                               B[g][:, :].rearrange("p (h q) -> p h q", q=P), ACT.Copy).then_inc(S["act_c_pT"], 1)
            def highs(e, i):
                for which in range(2):
                    for c in range(DC):
                        last = act.activation(high13[:, i, which, c, :], w13[which][:, e, c, :], ACT.Copy)
                    last.then_inc(S["act_m_high"], 1)

            act.wait_ge(S["experts_loaded"], 1)
            highs(0, 0)
            highs(1, 1)
            act.wait_ge(S["dve_m_sub"], 1)
            act.activation(small[:, 8:16], small[:, 8:16], ACT.Exp).then_inc(S["act_m_exp"], 1)

            def sigmoid(e, i):
                act.wait_ge(S["pe_m_h1"], e + 1)
                if not isinstance(e, int) or e >= 2:
                    act.wait_ge(S["dve_m_g"], e - 1)
                act.activation(sig[i], B[i][:, :], ACT.Sigmoid).then_inc(S["act_m_sig"], 1)

            def gated_out(e, i, loaded=None):
                if loaded is not None:
                    act.wait_ge(S["experts_loaded"], loaded)
                act.wait_ge(S["pe_m_gT"], e + 1)
                if not isinstance(e, int) or e >= 2:
                    act.wait_ge(S["pe_m_down"], e - 1)
                act.activation(gT[i], B[4 + i][:, :], ACT.Copy).then_inc(S["act_m_gT"], 1)

            sig = [sm[:, 4 * i:4 * i + 4, :].rearrange("p a b -> p (a b)") for i in range(2)]
            gT = [pT[:, 4 * i:4 * i + 4, :].rearrange("p a b -> p (a b)") for i in range(2)]
            sigmoid(0, 0)
            sigmoid(1, 1)
            gated_out(0, 0, 2)
            highs(2, 0)
            with act.Fori(1, EXPERTS // 2 - 1, 1) as m:
                for i in range(2):
                    sigmoid(m * 2 + i, i)
                    gated_out(m * 2 + (i - 1), 1 - i, m + (1 + i))
                    highs(m * 2 + (i + 1), 1 - i)
            sigmoid(EXPERTS - 2, 0)
            gated_out(EXPERTS - 3, 1, EXPERTS // 2)
            highs(EXPERTS - 1, 1)
            sigmoid(EXPERTS - 1, 1)
            gated_out(EXPERTS - 2, 0)
            gated_out(EXPERTS - 1, 1)

        @block.tensor
        def _(pe):
            def transpose_d(src, bank, done):
                for c in range(DC):
                    last = pe.transpose(bank[:, c * P:(c + 1) * P], src[:, c * P:(c + 1) * P], ident)
                last.then_inc(S[done], 1)

            def project(srcT, names, bank):
                for i, name in enumerate(names):
                    for c in range(DC):
                        last = pe.matmul(bank[:, i * D:(i + 1) * D], srcT[:, c, :], w[name][:, c, :],
                                         start=(c == 0), stop=(c == DC - 1))
                return last

            def keys_values(b, j, some=None):
                n = b * CHUNKS + j
                products = [(a, v, c) for a, v in ((0, 0), (1, 0), (0, 1)) for c in range(DC)]
                if some != 1:
                    pe.wait_ge(S["cl_ready"], n + 1)
                    if isinstance(b, int) and b == 0:
                        if j >= 2:
                            pe.wait_ge(S["kvf_ready"], n - 1)
                    elif j % CHUNKS == 2:
                        pe.wait_ge(S["kvf_ready"], n - 1)
                    elif j != 1 and j != CHUNKS + 1 and j > 0:
                        pe.wait_ge(S["kvf_ready"], n)
                bank = kv_of(b, j)
                for i, (a, v, c) in enumerate(products):
                    if some is None or i // (len(products) // 2) == some:
                        last = pe.matmul(bank[:, :], cparts[j % 2][:, a, c, :], wkv[:, v, c, :],
                                         start=(i == 0), stop=(i == len(products) - 1))
                if some != 0:
                    last.then_inc(S["kv_done"], 1)

            pe.wait_ge(S["ld_const"], 16)
            pe.wait_ge(S["dve_xn"], 1)
            transpose_d(xn, B[0], "pe_xnT")
            pe.wait_ge(S["dve_xnT"], 1)
            pe.wait_ge(S["ld_q"], 32)
            project(xnT, ["xq"], B[1]).then_inc(S["pe_q"], 1)
            pe.wait_ge(S["dve_wkvl"], 2)
            keys_values(0, 0)
            pe.wait_ge(S["dve_qparts"], 1)
            pe.wait_ge(S["dve_ident"], 1)
            pe.wait_ge(S["pool_setup"], 1)
            for g in range(GROUPS):
                for h in range(GH):
                    last = pe.transpose(B[2 + g][0:96, h * P:(h + 1) * P].bitcast(F32R), qparts[:, GH * g + h, :],
                                        ident_r[:, :])
                last.then_inc(S["pe_qT"], 1)

            def turn_keys(b, j, u):
                n = b * CHUNKS + j
                if u == 0:
                    pe.wait_ge(S["kl_ready"], n + 1)
                if u == 1 or not isinstance(b, int) or n > 0:
                    pe.wait_ge(S["kt_ready"], 2 * n + u)
                for p in range(PAIRS // 2):
                    last = pe.transpose(kt_bank[:, p * P:(p + 1) * P].bitcast(F32R),
                                        kparts[j % 2][:, u * (PAIRS // 2) + p, :], ident_r[:, :])
                last.then_inc(S["kt_done"], 1)

            def max_scores(b, s, v):
                m = b * (8 * STEPS) + (8 * s + v)
                pe.wait_ge(S["kt_ready"], b * (2 * CHUNKS) + 4 * s + (3 if v < 4 else 4))
                if not isinstance(b, int) or m >= 2:
                    pe.wait_ge(S["mx_read"], m - 1)
                for a in range(2):
                    last = pe.matmul(mx_bank[v % 2][:, a * 2 * P:(a + 1) * 2 * P], qmat[0:96, 2 * v + a, :],
                                     kT[0:96, s, v, :], start=True, stop=True)
                last.then_inc(S["mx_done"], 1)

            def turn_max(b):
                pe.wait_ge(S["mparts_ready"], b * 2 + 2)
                for i in range(2):
                    pe.transpose(mx_bank[i][:, 0:P].bitcast(F32R), maxparts[:, :], ident_r[:, :]
                                 ).then_inc(S["mt_done"], 1)

            def scores(c, k, kv=True):
                for k in (k, k + 1):
                    n, g = c * (CHUNKS * GROUPS) + k, k % GROUPS
                    if k == 1:
                        pe.wait_ge(S["qmat1_ready"], c + 1)
                    elif k < GROUPS:
                        pe.wait_ge(S["qmat_ready"], c * (GROUPS - 1) + max(1, g))
                    if k >= 3:
                        pe.wait_ge(S["exp_ready"], n - 2)
                    elif k == 2 and kv:
                        pe.wait_ge(S["kvf_ready"], c * CHUNKS + CHUNKS + 2)
                    j = k // GROUPS
                    for i in range(2):
                        p = 2 * g + i
                        last = pe.matmul(sc_bank[k % 3][:, i * 2 * P:(i + 1) * 2 * P],
                                         kT[:, j // 2, p, (j % 2) * P:(j % 2 + 1) * P],
                                         qmat[:, 2 * p:2 * p + 2, :], start=True, stop=True)
                    last.then_inc(S["sc_done"], 1)

            def weighted_values(c, k):
                for k in (k, k + 1):
                    j, g = k // GROUPS, k % GROUPS
                    if k == 0:
                        pe.wait_ge(S["part_ready"], c + 1)
                    pe.wait_ge(S["exp_ready"], c * (CHUNKS * GROUPS) + k + 1)
                    if g == 0:
                        pe.wait_ge(S["val_ready"], c * CHUNKS + (j + 1))
                    for r in range(GH):
                        last = pe.matmul(pv_bank[32 * r:32 * r + VW, g * P:(g + 1) * P], val[:, j, GH * g + r, :],
                                         probs[g][:, r, :], start=(k == 0), stop=(j == CHUNKS - 1),
                                         skip_group_check=True)
                    last.then_inc(S["pv_done"], 1)

            def quarter(b, s, i, first, last):
                k = 8 * s + 2 * i
                if not first:
                    scores(b - 1, k)
                if i > 0:
                    turn_keys(b, 2 * s + i // 2, i % 2)
                if not first and k > 0:
                    weighted_values(b - 1, k - 2)
                if i == 0:
                    turn_keys(b, 2 * s, 0)
                ms, v = (s, 2 * i - 4) if i >= 2 else (s - 1, 2 * i + 4)
                if ms >= 0 and i != 2:
                    max_scores(b, ms, v)
                if i == 0 and (s > 0 or first):
                    keys_values(b, 2 * s + (3 if first else 1))
                if i == 2:
                    j = 2 * s + (4 if first else 2)
                    project = first or s > 0 and not (last and s == STEPS - 1)
                    if project:
                        keys_values(b, j, 0)
                    max_scores(b, ms, v)
                    if project:
                        keys_values(b, j, 1)
                if ms >= 0:
                    max_scores(b, ms, v + 1)

            def steps(b, first, last):
                for s in range(STEPS):
                    for i in range(4):
                        quarter(b, s, i, first, last)
                if not (first or last):
                    keys_values(b, CHUNKS + 1, 0)
                max_scores(b, STEPS - 1, 4)
                max_scores(b, STEPS - 1, 5)
                if not (first or last):
                    keys_values(b, CHUNKS + 1, 1)
                max_scores(b, STEPS - 1, 6)
                max_scores(b, STEPS - 1, 7)
                if not first:
                    weighted_values(b - 1, 8 * STEPS - 2)
                if not (first or last):
                    keys_values(b, CHUNKS + 2)
                turn_max(b)

            keys_values(0, 1)
            keys_values(0, 2)
            pe.wait_ge(S["dve_pvzero"], 1)
            pe.wait_ge(S["dve_qmat"], 2)
            pe.wait_ge(S["act_qmat"], 2)
            steps(0, True, False)
            with pe.Fori(1, BLOCKS - 1, 1) as b:
                steps(b, False, False)
            steps(BLOCKS - 1, False, True)

            def turn_part(b):
                pe.wait_ge(S["part_ready"], b + 2)
                if b >= 2:
                    pe.wait_ge(S["dve_partT_read"], b - 1)
                for g in range(GROUPS):
                    last = pe.transpose(B[b % 2][:, g * P:(g + 1) * P], parts[:, b + 1, g * P:(g + 1) * P], ident)
                last.then_inc(S["pe_partT"], 1)

            for k in range(0, 8 * STEPS, 2):
                scores(BLOCKS - 1, k, False)
                if k % 8 == 4 and k // 8 < BLOCKS - 1:
                    turn_part(k // 8)
                if k > 0:
                    weighted_values(BLOCKS - 1, k - 2)
            weighted_values(BLOCKS - 1, 8 * STEPS - 2)

            turn_part(BLOCKS - 1)
            pe.wait_ge(S["dve_att"], 1)
            transpose_d(xn, B[0], "pe_attT")
            pe.wait_ge(S["dve_attT"], 1)
            pe.wait_ge(S["ld_small"], 16 * (len(WEIGHTS) - 3 + 3))
            project(xnT, ["xo"], B[1]).then_inc(S["pe_xo"], 1)

            pe.wait_ge(S["dve_a_xn"], 1)
            transpose_d(xn, B[0], "pe_a_xnT")
            pe.wait_ge(S["dve_a_xnT"], 1)
            project(xnT, ["aq", "ak"], B[1]).then_inc(S["pe_a_proj"], 1)
            project(xnT, ["av", "ag"], B[2]).then_inc(S["pe_a_proj"], 1)
            pe.wait_ge(S["dve_a_qkv"], 1)
            transpose_d(ta, B[3], "pe_a_qT")
            pe.wait_ge(S["dve_a_vg"], 1)
            for c in range(DC):
                pe.matmul(B[4][:, c * D:c * D + P], ta[:, D + c * P:D + (c + 1) * P], tb[:, c * P:(c + 1) * P],
                          start=True, stop=True)
                last = pe.matmul(B[4][:, c * D + P:c * D + P + 1], ta[:, D + c * P:D + (c + 1) * P], ones[:, :],
                                 start=True, stop=True)
            last.then_inc(S["pe_a_kv"], 1)
            pe.wait_ge(S["dve_a_kvr"], 1)
            for c in range(DC):
                last = pe.matmul(B[5][:, c * D:c * D + P + H // DC], xnT[:, c, :], kvr[:, c, :], start=True, stop=True)
            last.then_inc(S["pe_a_num"], 1)
            pe.wait_ge(S["dve_a_out"], 1)
            transpose_d(xn, B[0], "pe_a_outT")
            pe.wait_ge(S["dve_a_outT"], 1)
            project(xnT, ["ao"], B[1]).then_inc(S["pe_a_o"], 1)

            pe.wait_ge(S["dve_c_xn"], 1)
            transpose_d(xn, B[0], "pe_c_xnT")
            pe.wait_ge(S["dve_c_xnT"], 1)
            project(xnT, ["fq", "fk"], B[1]).then_inc(S["pe_c_proj"], 1)
            project(xnT, ["fv"], B[2]).then_inc(S["pe_c_proj"], 1)
            pe.wait_ge(S["dve_c_qk"], 1)
            for i in range(2):
                for c in range(DC):
                    at_column = (1 - i) * D + c * P
                    last = pe.transpose((B[3], B[5])[i][:, c * P:(c + 1) * P], ta[:, at_column:at_column + P], ident)
                last.then_inc(S["pe_c_qkT"], 1)
            for c in range(DC):
                for u in range(2):
                    if (c, u) == (0, 0):
                        pe.wait_ge(S["act_c_qT"], 1)
                    pe.wait_ge(S["dve_c_kbd"], 2 * c + u + 1)
                    pe.matmul(B[4 + 2 * c + u][:, :], xnT[:, c, :], kbd[:, c, GH * u:GH * (u + 1), :],
                              start=True, stop=True).then_inc(S["pe_c_scores"], 1)
            for g in range(GROUPS):
                pe.wait_ge(S["act_c_exp"], g + 1)
                for h in range(GH):
                    last = pe.transpose(B[g][:, h * P:(h + 1) * P], sm[:, GH * g + h, :], ident)
                last.then_inc(S["pe_c_pT"], 1)
            pe.wait_ge(S["dve_c_pT"], 2)
            pe.wait_ge(S["act_c_pT"], 2)
            for g in range(GROUPS):
                for r in range(GH):
                    last = pe.matmul(B[4][32 * r:32 * r + VW, g * P:(g + 1) * P], vaug[:, GH * g + r, :],
                                     pT[:, GH * g + r, :], start=True, stop=True)
            last.then_inc(S["pe_c_pv"], 1)
            pe.wait_ge(S["dve_c_oT"], 1)
            for g in range(GROUPS):
                last = pe.transpose(B[5][:, g * P:(g + 1) * P], oT[:, g, :], ident)
            last.then_inc(S["pe_c_o"], 1)
            pe.wait_ge(S["dve_c_att"], 1)
            transpose_d(xn, B[0], "pe_c_attT")
            pe.wait_ge(S["dve_c_attT"], 1)
            project(xnT, ["fo"], B[1]).then_inc(S["pe_c_proj_o"], 1)

            pe.wait_ge(S["dve_m_t"], 1)
            transpose_d(xn, B[0], "pe_m_tT")
            pe.wait_ge(S["dve_m_tT"], 1)
            for c in range(DC):
                last = pe.matmul(B[7][:, 0:EXPERTS], xnT[:, c, :], router[:, c, :], start=(c == 0), stop=(c == DC - 1))
            last.then_inc(S["pe_m_logits"], 1)

            def up(m, i, which):
                e = m * 2 + i
                if which == 0:
                    pe.wait_ge(S["experts_loaded"], m + 1)
                    if not isinstance(m, int) or m > 0:
                        pe.wait_ge(S["dve_m_g"], e - 1)
                pe.wait_ge(S["act_m_high"], 2 * e + (which + 1))
                products = [(a, low, c) for a, low in ((0, 0), (1, 0), (0, 1)) for c in range(DC)]
                for n, (a, low, c) in enumerate(products):
                    if (low, c) == (1, 0):
                        if isinstance(m, int) and m == 0:
                            pe.wait_ge(S["pool_m_low"], 2 * e + (which + 1))
                        else:
                            pe.wait_ge(S["dve_m_low"], 2 * e - 3 + which)
                    weights = (low13[which][:, e, c, :] if low else high13[:, i, which, c, :])
                    last = pe.matmul(B[2 * which + i][:, :], tparts[:, a, c, :], weights,
                                     start=(n == 0), stop=(n == len(products) - 1))
                last.then_inc(S[("pe_m_h1", "pe_m_h3")[which]], 1)

            def turn(e, i):
                pe.wait_ge(S["dve_m_g"], e + 1)
                if not isinstance(e, int) or e >= 2:
                    pe.wait_ge(S["act_m_gT"], e - 1)
                for k in range(IC):
                    last = pe.transpose(B[4 + i][:, k * P:(k + 1) * P], sm[:, 8 + 4 * i + k, :], ident)
                last.then_inc(S["pe_m_gT"], 1)

            def down(e, i, first, final):
                pe.wait_ge(S["act_m_gT"], e + 1)

                for k in range(IC):
                    last = pe.matmul(B[6][:, 0:D], pT[:, 4 * i + k, :], w2[:, e, k, :],
                                     start=(first and k == 0), stop=(final and k == IC - 1))
                last.then_inc(S["pe_m_down"], 1)
                if final:
                    return last

            pe.wait_ge(S["dve_m_tparts"], 1)
            up(0, 0, 0)
            up(0, 0, 1)
            up(0, 1, 0)
            turn(0, 0)
            up(0, 1, 1)
            down(0, 0, True, False)
            with pe.Fori(1, EXPERTS // 2, 1) as m:
                for i in range(2):
                    e = m * 2 + (i - 1)
                    up(m, i, 0)
                    turn(e, 1 - i)
                    up(m, i, 1)
                    down(e, 1 - i, False, False)
            turn(EXPERTS - 1, 1)
            down(EXPERTS - 1, 1, False, True)

        @block.vector
        def _(dve):
            links = [0]

            def link(ins):
                links[0] += 1
                ins.then_inc(S["dve_chain"], 1)
                dve.wait_ge(S["dve_chain"], links[0])

            def rsqrt(v, minus_half_v, y, tmp):
                link(dve.tensor_scalar(y.bitcast(I32), v.bitcast(I32), -0.5, float(0x5F3759DF), ALU.mult, ALU.add))
                for _ in range(3):
                    link(dve.scalar_tensor_tensor(tmp, y, y, minus_half_v, ALU.mult, ALU.mult))
                    link(dve.scalar_tensor_tensor(y, tmp, 1.5, y, ALU.add, ALU.mult))

            def layernorm(dst, src):
                link(dve.bn_stats(small[:, 0:6], src))
                link(dve.bn_aggr(small[:, 6:8], small[:, 0:6]))
                dve.tensor_scalar(small[:, 10:11], small[:, 7:8], EPS_LN, -0.5, ALU.add, ALU.mult)
                link(dve.tensor_scalar(small[:, 11:12], small[:, 7:8], EPS_LN, None, ALU.add))
                rsqrt(small[:, 11:12], small[:, 10:11], small[:, 8:9], small[:, 9:10])
                return dve.tensor_scalar(dst, src, small[:, 6:7], small[:, 8:9], ALU.subtract, ALU.mult)

            def rmsnorm(dst, src, weight, tmp):
                link(dve.tensor_tensor(tmp, src, src, ALU.mult))
                link(dve.tensor_reduce(small[:, 0:1], tmp, AX_X, ALU.add))
                dve.tensor_scalar(small[:, 4:5], small[:, 0:1], -0.5 / D, -0.5 * EPS_RMS, ALU.mult, ALU.add)
                link(dve.tensor_scalar(small[:, 1:2], small[:, 0:1], 1.0 / D, EPS_RMS, ALU.mult, ALU.add))
                rsqrt(small[:, 1:2], small[:, 4:5], small[:, 2:3], small[:, 3:4])
                return dve.scalar_tensor_tensor(dst, src, small[:, 2:3], weight, ALU.mult, ALU.mult)

            def turned(dst, bank, pe_signal, signal):
                dve.wait_ge(S[pe_signal], 1)
                dve.tensor_copy(dst[:, :, :], bank[:, 0:D].rearrange("p (c n) -> p c n", n=P)).then_inc(S[signal], 1)

            dve.memset(pv_bank[:, :], 0.0).then_inc(S["dve_pvzero"], 1)
            dve.wait_ge(S["ld_x"], 16)
            layernorm(xn[:, :], x[:, :]).then_inc(S["dve_xn"], 1)
            dve.wait_ge(S["ld_const"], 16)
            dve.tensor_copy(ident_r[:, :], ident).then_inc(S["dve_ident"], 1)
            turned(xnT, B[0], "pe_xnT", "dve_xnT")
            dve.wait_ge(S["act_wkvh"], 1)
            for i, name in enumerate(("xk", "xv")):
                dve.tensor_tensor(wkv[:, 1, :, i * D:(i + 1) * D], w[name][:, :, :],
                                  wkv[:, 0, :, i * D:(i + 1) * D].bitcast(F32), ALU.subtract
                                  ).then_inc(S["dve_wkvl"], 1)
            dve.wait_ge(S["ld_q"], 32)
            dve.memset(kbias[:, 1, :], 0.0)
            link(dve.tensor_copy(kbias[:, 0, :], bv("bxk")[:, 0, :]))
            dve.wait_ge(S["pe_q"], 1)
            q = parts[:, 0, 0:D]
            link(dve.tensor_tensor(q, B[1][:, 0:D], bv("bxq")[:, 0, :], ALU.add))
            dve.wait_ge(S["pool_setup"], 1)
            q4 = q.rearrange("p (m a d) -> p m a d", a=2, d=HD)
            qp4 = qparts[:, :, :].rearrange("p (m a) c -> p m a c", a=2)
            for seg in (0, 32):
                for a in range(2):
                    last = dve.tensor_scalar(qp4[:, :, a, seg + HD * a:seg + HD * (a + 1)], q4[:, :, a, :],
                                             SCALE, None, ALU.mult)
            link(last)
            for a in range(2):
                last = dve.scalar_tensor_tensor(qp4[:, :, a, 64 + HD * a:64 + HD * (a + 1)], q4[:, :, a, :], SCALE,
                                                qp4[:, :, a, HD * a:HD * (a + 1)].bitcast(F32), ALU.mult, ALU.subtract)
            last.then_inc(S["dve_qparts"], 1)
            for g in (0, 2):
                dve.wait_ge(S["pe_qT"], g + 1)
                dve.tensor_copy(qmat[0:96, GH * g:GH * (g + 1), :],
                                B[2 + g][0:96, :].rearrange("p (h q) -> p h q", q=P)).then_inc(S["dve_qmat"], 1)
            def kv_out(b, j):
                n, i = b * CHUNKS + j, j % 2
                dve.wait_ge(S["kv_done"], n + 1)
                if not isinstance(n, int) or n >= 2:
                    dve.wait_ge(S["val_ready"], n - 1)
                    dve.wait_ge(S["kl_ready"], n - 1)
                dve.tensor_tensor(kvf[i][:, :, :], kv_of(b, j)[:, :].rearrange("p (s n) -> p s n", s=2),
                                  kbias[:, :, :], ALU.add).then_inc(S["kvf_ready"], 1)

            def keys_out(b, j, u):
                dve.wait_ge(S["kt_done"], b * (2 * CHUNKS) + (2 * j + u + 1))
                dve.tensor_copy(kT[:, j // 2, 4 * u:4 * u + 4, (j % 2) * P:(j % 2 + 1) * P],
                                kt_bank[:, :].rearrange("p (a k) -> p a k", k=P)).then_inc(S["kt_ready"], 1)

            def step_max(b, s, v):
                dve.wait_ge(S["mx_done"], b * (8 * STEPS) + (8 * s + v + 1))
                dve.tensor_reduce(stepmax[:, s, 2 * v:2 * v + 2],
                                  mx_bank[v % 2][:, :].rearrange("p (a k) -> p a k", a=2), AX_X, ALU.max
                                  ).then_inc(S["mx_read"], 1)

            def block_max(b):
                dve.wait_ge(S["mx_read"], b * (8 * STEPS) + 8 * STEPS)
                dve.tensor_reduce(curmax[:, :], stepmax[:, :, :].rearrange("p s h -> p h s"), AX_X, ALU.max
                                  ).then_inc(S["curmax_ready"], 1)
                dve.wait_ge(S["curmax_ready"], b + 1)
                dve.tensor_scalar(maxparts[:, 96:96 + H], curmax[:, :], -1.0, None, ALU.mult
                                  ).then_inc(S["mparts_ready"], 1)
                dve.wait_ge(S["mparts_ready"], b * 2 + 1)
                dve.scalar_tensor_tensor(maxparts[:, 96 + H:P], curmax[:, :], -1.0,
                                         maxparts[:, 96:96 + H].bitcast(F32), ALU.mult, ALU.subtract
                                         ).then_inc(S["mparts_ready"], 1)
                dve.tensor_scalar(bmax[:, b, :], curmax[:, :], 1.0, None, ALU.mult).then_inc(S["bmax_ready"], 1)

            def max_rows(b, g):
                if g == 0:
                    dve.wait_ge(S["mt_done"], b * 2 + 1)
                dve.tensor_tensor(qmat[96:P, GH * g:GH * (g + 1), :],
                                  over_heads(mx_bank[0][96:P, 0:P], GH),
                                  per_head(const[96:P, C_MM + GH * g:C_MM + GH * (g + 1)], P), ALU.mult
                                  ).then_inc(S["qmat_ready"], 1)

            def quarter(b, s, i, first, last):
                if not (first or s == STEPS - 1 and i == 3):
                    keys_out(b, 2 * s + i // 2, i % 2)
                ms, v = (s, 2 * i - 4) if i >= 2 else (s - 1, 2 * i + 4)
                if ms >= 0 and i != 2:
                    step_max(b, ms, v)
                if i == 0 and (s > 0 or first):
                    kv_out(b, 2 * s + (2 if first else 1))
                if i == 2:
                    step_max(b, ms, v)
                    if not (last and s == STEPS - 1):
                        kv_out(b, 2 * s + (3 if first else 2))
                if ms >= 0:
                    step_max(b, ms, v + 1)

            def steps(b, first, last):
                for s in range(STEPS):
                    for i in range(4):
                        quarter(b, s, i, first, last)
                for v in range(4, 8):
                    step_max(b, STEPS - 1, v)
                block_max(b)
                if not (first or last):
                    kv_out(b, CHUNKS + 1)
                for g in (0, 2, 3):
                    max_rows(b, g)

            kv_out(0, 0)
            kv_out(0, 1)
            steps(0, True, False)
            with dve.Fori(1, BLOCKS - 1, 1) as b:
                steps(b, False, False)
            steps(BLOCKS - 1, False, True)

            dve.wait_ge(S["bmax_ready"], BLOCKS)
            link(dve.tensor_reduce(small[:, 16:32], bmax[:, :, :].rearrange("p b h -> p h b"), AX_X, ALU.max))
            dve.tensor_tensor(bmax[:, :, :], bmax[:, :, :], over_heads(small[:, 16:32], BLOCKS), ALU.subtract
                              ).then_inc(S["dve_dmax"], 1)
            dve.wait_ge(S["act_bw"], 1)
            merged = parts[:, 0, 0:H * VW].rearrange("p (h v) -> p h v", v=VW)
            piece = small[:, 224:224 + H * VW].rearrange("p (h v) -> p h v", v=VW)
            for b in range(BLOCKS):
                dve.wait_ge(S["pe_partT"], b + 1)
                bank = B[b % 2][:, :].rearrange("p (h v) -> p h v", v=32)[:, :, 0:VW]
                ins = dve.tensor_tensor(merged if b == 0 else piece, bank, per_head(bmax[:, b, :], VW), ALU.mult)
                ins.then_inc(S["dve_partT_read"], 1)
                dve.wait_ge(S["dve_partT_read"], b + 1)
                if b:
                    link(dve.tensor_tensor(merged, merged, piece, ALU.add))
            link(dve.reciprocal(small[:, 32:48], merged[:, :, HD]))
            dve.tensor_tensor(xn[:, :].rearrange("p (h d) -> p h d", d=HD), merged[:, :, 0:HD],
                              per_head(small[:, 32:48], HD), ALU.mult).then_inc(S["dve_att"], 1)
            turned(xnT, B[0], "pe_attT", "dve_attT")
            link(dve.tensor_tensor(x1[:, :], x[:, :], bv("bxo")[:, 0, :], ALU.add))
            dve.wait_ge(S["pe_xo"], 1)
            link(dve.tensor_tensor(x1[:, :], B[1][:, 0:D], x1[:, :], ALU.add))

            layernorm(xn[:, :], x1[:, :]).then_inc(S["dve_a_xn"], 1)
            turned(xnT, B[0], "pe_a_xnT", "dve_a_xnT")
            dve.wait_ge(S["pe_a_proj"], 1)
            link(dve.tensor_tensor(ta[:, :].rearrange("p (s n) -> p s n", s=2),
                                   B[1][:, :].rearrange("p (s n) -> p s n", s=2), bv("baq", 2), ALU.add))
            dve.tensor_scalar(tc[:, :], ta[:, :], 0.0, None, ALU.min).then_inc(S["dve_a_neg"], 1)
            dve.wait_ge(S["act_a_exp"], 1)
            dve.scalar_tensor_tensor(ta[:, :], ta[:, :], 0.0, tc[:, :], ALU.max, ALU.add).then_inc(S["dve_a_qkv"], 1)
            dve.wait_ge(S["pe_a_proj"], 2)
            dve.tensor_tensor(tb[:, :].rearrange("p (s n) -> p s n", s=2),
                              B[2][:, :].rearrange("p (s n) -> p s n", s=2), bv("bav", 2), ALU.add
                              ).then_inc(S["dve_a_vg"], 1)
            dve.wait_ge(S["pe_a_qT"], 1)
            dve.tensor_copy(xnT[:, :, :], B[3][:, 0:D].rearrange("p (c n) -> p c n", n=P))
            dve.wait_ge(S["act_a_exp"], 2)
            link(dve.tensor_scalar(tb[:, D:2 * D], tb[:, D:2 * D], 1.0, None, ALU.add))
            dve.reciprocal(tc[:, 0:P], tb[:, D:D + P])
            dve.wait_ge(S["pe_a_kv"], 1)
            for c in range(DC):
                dve.tensor_tensor(kvr[:, c, 0:P], B[4][:, c * D:c * D + P], const[:, C_BM:C_BM + P], ALU.mult)
                last = dve.tensor_scalar(kvr[:, c, P:P + H // DC], const[:, C_HM:C_HM + H // DC],
                                         B[4][:, c * D + P:c * D + P + 1], None, ALU.mult)
            last.then_inc(S["dve_a_kvr"], 1)
            dve.reciprocal(tc[:, P:D], tb[:, D + P:2 * D])
            dve.wait_ge(S["pe_a_num"], 1)
            num = B[5][:, :].rearrange("p (c n) -> p c n", c=DC)
            zz = small[:, 16:32].rearrange("p (c h) -> p c h", c=DC)
            link(dve.tensor_scalar(zz, num[:, :, P:P + H // DC], EPS_Z, None, ALU.add))
            link(dve.reciprocal(small[:, 32:48], small[:, 16:32]))
            for c in range(DC):
                last = dve.tensor_tensor(ta[:, c * P:(c + 1) * P].rearrange("p (h d) -> p h d", d=HD),
                                         num[:, c, 0:P].rearrange("p (h d) -> p h d", d=HD),
                                         per_head(small[:, 32 + 8 * c:40 + 8 * c], HD), ALU.mult)
            link(last)
            dve.tensor_tensor(xn[:, :], ta[:, 0:D], tc[:, 0:D], ALU.mult).then_inc(S["dve_a_out"], 1)
            turned(xnT, B[0], "pe_a_outT", "dve_a_outT")
            link(dve.tensor_tensor(x2[:, :], x1[:, :], bv("bao")[:, 0, :], ALU.add))
            dve.wait_ge(S["pe_a_o"], 1)
            link(dve.tensor_tensor(x2[:, :], B[1][:, 0:D], x2[:, :], ALU.add))

            link(layernorm(xl[:, :], x2[:, :]))
            rmsnorm(xn[:, :], xl[:, :], bv("anw")[:, 0, :], tb[:, 0:D]).then_inc(S["dve_c_xn"], 1)
            turned(xnT, B[0], "pe_c_xnT", "dve_c_xnT")
            dve.memset(vaug[:, :, HD:VW], 1.0)
            dve.wait_ge(S["pe_c_proj"], 1)
            pairs = B[1][:, :].rearrange("p (h j e) -> p h j e", h=2 * H, e=2)
            turnedqk = ta[:, :].rearrange("p (h j e) -> p h j e", h=2 * H, e=2)
            fr = freqs[:, :].rearrange("p (j e) -> p j e", e=2)
            cos, sin = (over_heads(fr[:, :, e], 2 * H) for e in range(2))
            t0, t1, t2, t3 = (v.rearrange("p (h j) -> p h j", j=HD // 2)
                              for v in (tb[:, 0:D], tb[:, D:2 * D], tc[:, 0:D], tc[:, D:2 * D]))
            dve.tensor_tensor(t0, pairs[:, :, :, 0], cos, ALU.mult)
            dve.tensor_tensor(t1, pairs[:, :, :, 1], sin, ALU.mult)
            dve.tensor_tensor(t2, pairs[:, :, :, 0], sin, ALU.mult)
            link(dve.tensor_tensor(t3, pairs[:, :, :, 1], cos, ALU.mult))
            dve.tensor_tensor(turnedqk[:, :, :, 0], t0, t1, ALU.subtract)
            dve.tensor_tensor(turnedqk[:, :, :, 1], t2, t3, ALU.add).then_inc(S["dve_c_qk"], 1)
            dve.wait_ge(S["pe_c_proj"], 2)
            dve.tensor_copy(vaug[:, :, 0:HD], B[2][:, 0:D].rearrange("p (h d) -> p h d", d=HD)
                            )
            dve.wait_ge(S["pe_c_qkT"], 1)
            for c in range(DC):
                for u in range(2):
                    dve.tensor_tensor(kbd[:, c, GH * u:GH * (u + 1), :], over_heads(B[3][:, c * P:(c + 1) * P], GH),
                                      per_head(const[:, C_HM + GH * u:C_HM + GH * (u + 1)], P), ALU.mult
                                      ).then_inc(S["dve_c_kbd"], 1)

            def masked(g):
                dve.wait_ge(S["pe_c_scores"], g + 1)
                dve.tensor_tensor(sm[:, GH * g:GH * (g + 1), :], B[4 + g][:, :].rearrange("p (h k) -> p h k", k=P),
                                  over_heads(const[:, C_CA:C_CA + P], GH), ALU.add).then_inc(S["dve_c_masked"], 1)

            def row_max(g):
                dve.wait_ge(S["dve_c_masked"], g + 1)
                dve.tensor_reduce(small[:, 16 + GH * g:16 + GH * (g + 1)], sm[:, GH * g:GH * (g + 1), :], AX_X, ALU.max
                                  ).then_inc(S["dve_c_max"], 1)

            def minus_max(g):
                dve.wait_ge(S["dve_c_max"], g + 1)
                dve.tensor_scalar(small[:, 48 + GH * g:48 + GH * (g + 1)], small[:, 16 + GH * g:16 + GH * (g + 1)],
                                  -SCALE, None, ALU.mult).then_inc(S["dve_c_sub"], 1)

            masked(0)
            for g in range(GROUPS):
                row_max(g)
                if g < GROUPS - 1:
                    masked(g + 1)
                minus_max(g)
            for g in (0, 2):
                dve.wait_ge(S["pe_c_pT"], g + 1)
                dve.tensor_copy(pT[:, GH * g:GH * (g + 1), :],
                                B[g][:, :].rearrange("p (h q) -> p h q", q=P)).then_inc(S["dve_c_pT"], 1)
            dve.wait_ge(S["pe_c_pv"], 1)
            dve.tensor_copy(oT[:, :, :], B[4][:, :].rearrange("p (g q) -> p g q", q=P)).then_inc(S["dve_c_oT"], 1)
            dve.wait_ge(S["pe_c_o"], 1)
            o = B[5][:, :].rearrange("p (h v) -> p h v", v=32)
            link(dve.reciprocal(small[:, 32:48], o[:, :, HD]))
            dve.tensor_tensor(xn[:, :].rearrange("p (h d) -> p h d", d=HD), o[:, :, 0:HD],
                              per_head(small[:, 32:48], HD), ALU.mult).then_inc(S["dve_c_att"], 1)
            turned(xnT, B[0], "pe_c_attT", "dve_c_attT")
            dve.wait_ge(S["pe_c_proj_o"], 1)
            link(dve.tensor_tensor(hres[:, :], B[1][:, 0:D], xl[:, :], ALU.add))

            rmsnorm(xn[:, :], hres[:, :], bv("fnw")[:, 0, :], tb[:, 0:D]).then_inc(S["dve_m_t"], 1)
            turned(xnT, B[0], "pe_m_tT", "dve_m_tT")
            link(dve.tensor_copy(tparts[:, 0, :, :], B[0][:, 0:D].rearrange("p (c n) -> p c n", n=P)))
            dve.tensor_tensor(tparts[:, 1, :, :], B[0][:, 0:D].rearrange("p (c n) -> p c n", n=P),
                              tparts[:, 0, :, :].bitcast(F32), ALU.subtract).then_inc(S["dve_m_tparts"], 1)
            link(dve.tensor_tensor(hres[:, :], hres[:, :], x2[:, :], ALU.add))
            dve.wait_ge(S["pe_m_logits"], 1)
            E = EXPERTS
            link(dve.tensor_reduce(small[:, 0:1], B[7][:, 0:E], AX_X, ALU.max))
            dve.tensor_scalar(small[:, 8:16], B[7][:, 0:E], small[:, 0:1], None, ALU.subtract
                              ).then_inc(S["dve_m_sub"], 1)
            dve.wait_ge(S["act_m_exp"], 1)
            pr = small[:, 16:24]
            link(dve.tensor_reduce(small[:, 1:2], small[:, 8:16], AX_X, ALU.add))
            link(dve.reciprocal(small[:, 2:3], small[:, 1:2]))
            link(dve.tensor_scalar(pr, small[:, 8:16], small[:, 2:3], None, ALU.mult))
            big = small[:, 64:128].rearrange("p (a b) -> p a b", b=E)
            same = small[:, 128:192].rearrange("p (a b) -> p a b", b=E)
            dve.tensor_tensor(big, over_heads(pr, E), per_head(pr, E), ALU.is_gt)
            link(dve.tensor_tensor(same, over_heads(pr, E), per_head(pr, E), ALU.is_equal))
            link(dve.tensor_tensor(same, same, const[:, C_LT:C_LT + E * E].rearrange("p (a b) -> p a b", b=E),
                                   ALU.mult))
            link(dve.tensor_tensor(big, big, same, ALU.add))
            link(dve.tensor_reduce(small[:, 24:32], big, AX_X, ALU.add))
            link(dve.scalar_tensor_tensor(small[:, 32:40], small[:, 24:32], 1.5, pr, ALU.is_lt, ALU.mult))
            link(dve.tensor_reduce(small[:, 3:4], small[:, 32:40], AX_X, ALU.add))
            link(dve.reciprocal(small[:, 4:5], small[:, 3:4]))
            link(dve.tensor_scalar(share[:, :, 0], small[:, 32:40], small[:, 4:5], None, ALU.mult))

            def low(e, i, which):
                dve.wait_ge(S["act_m_high"], 2 * e + (which + 1))
                dve.tensor_tensor(low13[which][:, e, :, :], w13[which][:, e, :, :],
                                  high13[:, i, which, :, :].bitcast(F32), ALU.subtract
                                  ).then_inc(S["dve_m_low"], 1)

            def gated(e, i, lows=True):
                sig = sm[:, 4 * i:4 * i + 4, :].rearrange("p a b -> p (a b)")
                g = sm[:, 8 + 4 * i:12 + 4 * i, :].rearrange("p a b -> p (a b)")
                dve.wait_ge(S["act_m_sig"], e + 1)
                if not isinstance(e, int) or e >= 2:
                    dve.wait_ge(S["pe_m_gT"], e - 1)
                dve.tensor_tensor(sig, sig, B[i][:, :], ALU.mult).then_inc(S["dve_m_w"], 1)
                if lows:
                    low(e + 1, 1 - i, 0)
                dve.wait_ge(S["dve_m_w"], e + 1)
                dve.wait_ge(S["pe_m_h3"], e + 1)
                dve.scalar_tensor_tensor(g, sig, share[:, e, :], B[2 + i][:, :], ALU.mult, ALU.mult
                                         ).then_inc(S["dve_m_g"], 1)
                if lows:
                    low(e + 1, 1 - i, 1)

            gated(0, 0, False)
            gated(1, 1)
            with dve.Fori(1, EXPERTS // 2 - 1, 1) as m:
                gated(m * 2, 0)
                gated(m * 2 + 1, 1)
            gated(EXPERTS - 2, 0)
            gated(EXPERTS - 1, 1, False)
            dve.wait_ge(S["pe_m_down"], EXPERTS)
            dve.tensor_tensor(fin[:, :], B[6][:, 0:D], hres[:, :], ALU.add).then_inc(S["dve_fin"], 1)


MATRICES = {"w_xq": ("L0_xattn_Wq", True), "w_xk": ("L0_xattn_Wk", True), "w_xv": ("L0_xattn_Wv", True),
            "w_xo": ("L0_xattn_Wo", True), "w_aq": ("L0_attn_wq_w", False), "w_ak": ("L0_attn_wk_w", False),
            "w_av": ("L0_attn_wv_w", False), "w_ag": ("L0_attn_wg_w", False), "w_ao": ("L0_attn_out_w", False),
            "w_fq": ("L0_ffn_wq", False), "w_fk": ("L0_ffn_wk", False), "w_fv": ("L0_ffn_wv", False),
            "w_fo": ("L0_ffn_wo", False), "router": ("L0_ffn_router_w", False), "freqs": ("L0_ffn_freqs_cis", False),
            "w1": ("L0_ffn_w1", False), "w3": ("L0_ffn_w3", False), "w2": ("L0_ffn_w2", False)}
VECTORS = {"bxq": "L0_xattn_bq", "bxk": "L0_xattn_bk", "bxv": "L0_xattn_bv", "bxo": "L0_xattn_bo",
           "baq": "L0_attn_wq_b", "bak": "L0_attn_wk_b", "bav": "L0_attn_wv_b", "bag": "L0_attn_wg_b",
           "bao": "L0_attn_out_b", "anw": "L0_ffn_attn_norm_w", "fnw": "L0_ffn_ffn_norm_w"}


def constants(np):
    c = np.zeros((P, C_N), np.float32)
    i = np.arange(P)
    c[:, C_ID:C_ID + P] = np.eye(P)
    c[:, C_BM:C_BM + P] = i[:, None] // HD == i[None, :] // HD
    c[:, C_CA:C_CA + P] = np.where(i[:, None] >= i[None, :], 0.0, MASKED)
    c[:, C_HM:C_HM + P // HD] = i[:, None] // HD == np.arange(P // HD)[None, :]
    c[96:, C_MM:C_MM + H] = np.arange(32)[:, None] % H == np.arange(H)[None, :]
    e = np.arange(EXPERTS)
    c[:, C_LT:] = (e[None, :] < e[:, None]).reshape(1, -1)
    return c


def kernel(**inputs):
    import numpy as np
    import concourse.bacc as bacc
    from concourse.bass_utils import run_bass_kernel_spmd

    nc = bacc.Bacc("TRN2", target_bir_lowering=False, num_devices=1)
    arrays = {"x": np.asarray(inputs["x"]).reshape(P, D), "const": constants(np)}
    c = np.asarray(inputs["ctx_1024"]).reshape(BLOCKS, 2, HALF, P, DC, P)
    arrays["ctxT"] = c.transpose(0, 1, 5, 2, 4, 3).reshape(BLOCKS, 2, P, HALF * DC * P)
    for name, (given, turned) in MATRICES.items():
        a = np.asarray(inputs[given])
        arrays[name] = a.T if turned else a
    arrays["biases"] = np.concatenate([np.asarray(inputs[VECTORS[name]]) for name in BIASES])
    arrays = {n: np.ascontiguousarray(a) for n, a in arrays.items()}
    dr = {n: nc.dram_tensor(f"in_{n}", a.shape, mybir.dt.from_np(a.dtype), kind="ExternalInput").ap()
          for n, a in arrays.items()}
    out = nc.dram_tensor("out", (P, D), F32, kind="ExternalOutput").ap()
    perceiver_layer(nc, dr, out)
    r = run_bass_kernel_spmd(nc, [{f"in_{n}": a for n, a in arrays.items()}], core_ids=[0])
    return r.results[0]["out"].reshape(1, P, D)
```
